# Optimizing a Trainium2 kernel written in Bass

```python
import numpy as np
import jax
import jax.numpy as jnp

def _softmax(x, axis=-1):
    return jax.nn.softmax(x, axis=axis)

def _gelu(x):
    return jax.nn.gelu(x, approximate=True)

def _silu(x):
    return jax.nn.silu(x)

def _sigmoid(x):
    return jax.nn.sigmoid(x)

def _layernorm(x, axis=-1, eps=1e-05):
    m = jnp.mean(x, axis=axis, keepdims=True)
    v = jnp.var(x, axis=axis, keepdims=True)
    return (x - m) / jnp.sqrt(v + eps)

def _scatter_add(tgt, idx, src, axis=0):
    return tgt.at[idx].add(src)

def _segment_sum(src, seg, n):
    return jax.ops.segment_sum(src, seg, n)
kernel_name = 'mk_flamingo_gated_d1_seqx_r4_d38833'

def setup_inputs(seed: int=0):
    np.random.seed(seed)
    _w = jnp.asarray

    def _rec_inputs():
        import jax
        import jax.numpy as jnp
        _rk = jax.random.key(seed)
        x = 0.5 + 0.2887 * jax.random.normal(jax.random.fold_in(_rk, 1), (4, 512, 512), jnp.float32)
        _lenS = 512 - jax.random.randint(jax.random.fold_in(_rk, 7), (4,), 0, max(1, 512 // 4) + 1, jnp.int32)
        _lenS2 = 512 - jax.random.randint(jax.random.fold_in(_rk, 8), (4,), 0, max(1, 512 // 4) + 1, jnp.int32)
        _ctx_512P = jax.random.normal(jax.random.fold_in(_rk, 11), (4, 16, 128), jnp.float32)
        _ctx_512c = jax.random.dirichlet(jax.random.fold_in(_rk, 511), 0.3 * jnp.ones((16,), jnp.float32), (4, 512))
        _ctx_512t = jnp.einsum('bsk,bkd->bsd', _ctx_512c, _ctx_512P)
        _ctx_512t = _ctx_512t * jax.lax.rsqrt(jnp.mean(jnp.square(_ctx_512t)) + 1e-12) * 0.953939
        ctx_512 = 7.22013e-05 + 1.00017 * (_ctx_512t + 0.3 * jax.random.normal(jax.random.fold_in(_rk, 611), (4, 512, 128), jnp.float32))
        _validS = jnp.arange(512)[None, :] < _lenS[:, None]
        _validS2 = jnp.arange(512)[None, :] < _lenS2[:, None]
        _causal = jnp.tril(jnp.ones((512, 512), dtype=bool))
        mask_SxS2_bk1 = jnp.broadcast_to(_validS2[0:1, :], (512, 512))
        mask_BxS2_bf0 = jnp.logical_not(jnp.ones((4, 512), dtype=bool))
        _g = jax.random.normal(jax.random.fold_in(_rk, 9001), (2, 1), jnp.float32)
        _g = jnp.sign(_g) * jnp.maximum(jnp.abs(_g), 1.0) + (_g == 0) * 1.0
        g_xattn = _g[0]
        g_ffn = _g[1]
        return (x, ctx_512, mask_SxS2_bk1, mask_BxS2_bf0, g_xattn, g_ffn)
    x, ctx_512, mask_SxS2_bk1, mask_BxS2_bf0, g_xattn, g_ffn = _rec_inputs()

    def _L0_xattn_setup():
        import jax, jax.numpy as jnp
        import numpy as np
        B, S, H = (8, 512, 128)
        key = jax.random.key(seed)
        kq, kk, kqc, kwq, kwk = jax.random.split(key, 5)
        q = jax.random.normal(kq, (B, S, H), dtype=jnp.float32)
        k = jax.random.normal(kk, (B, S, H), dtype=jnp.float32)
        qc_score = jax.random.uniform(kqc, (B, S, S), dtype=jnp.float32)
        attn_mask = jnp.triu(jnp.ones((S, S), dtype=bool), k=1)
        key_padding_mask = jnp.zeros((B, S), dtype=bool)
        scale = 1.0 / np.sqrt(H)
        Wq = jax.random.normal(kwq, (H, H), dtype=jnp.float32) * scale
        Wk = jax.random.normal(kwk, (H, H), dtype=jnp.float32) * scale
        bq = jnp.zeros((H,), dtype=jnp.float32)
        bk = jnp.zeros((H,), dtype=jnp.float32)
        return {'q': q, 'k': k, 'attn_mask': attn_mask, 'key_padding_mask': key_padding_mask, 'qc_score': qc_score, 'Wq': Wq, 'bq': bq, 'Wk': Wk, 'bk': bk}
    _L0_xattn_all = _L0_xattn_setup()
    _L0_xattn_in = {k: v for k, v in _L0_xattn_all.items() if k in ('Wq', 'bq', 'Wk', 'bk')}
    del _L0_xattn_all

    def _L0_ffn_setup():
        import jax, jax.numpy as jnp
        import numpy as np
        B, S, H = (2, 512, 512)
        FFN = 256
        E = 8
        TOP_K = 2
        key = jax.random.key(seed)
        ks = jax.random.split(key, 5)
        scale = 0.02
        hidden_states = jax.random.normal(ks[0], (B, S, H), dtype=jnp.float32)
        Wg = jax.random.normal(ks[1], (E, H), dtype=jnp.float32) * scale
        W1 = jax.random.normal(ks[2], (E, FFN, H), dtype=jnp.float32) * scale
        W3 = jax.random.normal(ks[3], (E, FFN, H), dtype=jnp.float32) * scale
        W2 = jax.random.normal(ks[4], (E, H, FFN), dtype=jnp.float32) * scale
        bias = jnp.zeros((E,), dtype=jnp.float32)
        return {'hidden_states': hidden_states, 'Wg': Wg, 'W1': W1, 'W2': W2, 'W3': W3, 'bias': bias}
    _L0_ffn_all = _L0_ffn_setup()
    _L0_ffn_in = {k: v for k, v in _L0_ffn_all.items() if k in ('Wg', 'W1', 'W2', 'W3', 'bias')}
    del _L0_ffn_all
    return {'x': x, 'ctx_512': ctx_512, 'mask_SxS2_bk1': mask_SxS2_bk1, 'mask_BxS2_bf0': mask_BxS2_bf0, 'g_xattn': g_xattn, 'g_ffn': g_ffn, 'L0_xattn_Wq': _L0_xattn_in['Wq'], 'L0_xattn_bq': _L0_xattn_in['bq'], 'L0_xattn_Wk': _L0_xattn_in['Wk'], 'L0_xattn_bk': _L0_xattn_in['bk'], 'L0_ffn_Wg': _L0_ffn_in['Wg'], 'L0_ffn_W1': _L0_ffn_in['W1'], 'L0_ffn_W2': _L0_ffn_in['W2'], 'L0_ffn_W3': _L0_ffn_in['W3'], 'L0_ffn_bias': _L0_ffn_in['bias']}

def reference(x, ctx_512, mask_SxS2_bk1, mask_BxS2_bf0, g_xattn, g_ffn, L0_xattn_Wq, L0_xattn_bq, L0_xattn_Wk, L0_xattn_bk, L0_ffn_Wg, L0_ffn_W1, L0_ffn_W2, L0_ffn_W3, L0_ffn_bias):
    import jax
    import jax.numpy as jnp

    def _L0_xattn_ref(q, k, attn_mask, key_padding_mask, qc_score, Wq, bq, Wk, bk):
        import jax, jax.numpy as jnp
        import numpy as np
        B, S, H = (8, 512, 128)
        qp = jnp.einsum('bsh,oh->bso', q, Wq) + bq
        kp = jnp.einsum('bth,oh->bto', k, Wk) + bk
        scaling = jnp.asarray(float(H) ** (-0.5), dtype=qp.dtype)
        scores = jnp.einsum('bsh,bth->bst', qp, kp) * scaling
        scores = scores * qc_score
        mask = attn_mask[None, :, :] | key_padding_mask[:, None, :]
        scores = jnp.where(mask, -jnp.inf, scores)
        return jax.nn.softmax(scores, axis=-1)

    def _L0_ffn_ref(hidden_states, Wg, W1, W2, W3, bias):
        import jax, jax.numpy as jnp
        import numpy as np
        B, S, H = (2, 512, 512)
        FFN = 256
        E = 8
        TOP_K = 2
        bsz, seq_len, hidden_dim = hidden_states.shape
        x = hidden_states.reshape(-1, hidden_dim)
        router_logits = x @ Wg.T
        routing_weights = jax.nn.sigmoid(router_logits.astype(jnp.float32))
        scores = routing_weights + bias
        _, top_k_index = jax.lax.top_k(scores, TOP_K)
        top_k_weights = jnp.take_along_axis(routing_weights, top_k_index, axis=1)
        top_k_weights = top_k_weights / top_k_weights.sum(axis=-1, keepdims=True)
        top_k_weights = top_k_weights.astype(x.dtype)
        one_hot = jax.nn.one_hot(top_k_index, Wg.shape[0], dtype=x.dtype)
        expert_w = jnp.einsum('tk,tke->te', top_k_weights, one_hot)
        h1 = jnp.einsum('th,efh->tef', x, W1)
        h3 = jnp.einsum('th,efh->tef', x, W3)
        g = jax.nn.silu(h1) * h3 * expert_w[:, :, None]
        out = jnp.einsum('tef,ehf->th', g, W2)
        return out.reshape(bsz, seq_len, hidden_dim)
    x = x + jnp.tanh(g_xattn[0]) * _L0_xattn_ref(ctx_512, ctx_512, mask_SxS2_bk1, mask_BxS2_bf0, _layernorm(x, axis=-1), L0_xattn_Wq, L0_xattn_bq, L0_xattn_Wk, L0_xattn_bk)
    x = x + jnp.tanh(g_ffn[0]) * _L0_ffn_ref(_layernorm(x, axis=-1), L0_ffn_Wg, L0_ffn_W1, L0_ffn_W2, L0_ffn_W3, L0_ffn_bias)
    return x

_drawn_inputs = setup_inputs


def setup_inputs(seed=0):
    import zlib

    import numpy as np

    out = dict(_drawn_inputs(seed))
    spreads = {'L0_xattn_bq': (0.0, 2.0), 'L0_xattn_bk': (0.0, 2.0), 'L0_ffn_bias': (0.0, 0.1)}
    factors = {'ctx_512': 3.19, 'L0_xattn_Wq': 3.148, 'L0_xattn_Wk': 2.993}
    for name, (base, spread) in spreads.items():
        noise = np.random.default_rng([zlib.crc32(name.encode()), seed]).standard_normal(out[name].shape)
        drawn = base * np.exp(spread * noise) if base else spread * noise
        out[name] = jnp.asarray(drawn.astype(out[name].dtype))
    for name, factor in factors.items():
        out[name] = (out[name] * factor).astype(out[name].dtype)
    return out
```

```python
from contextlib import ExitStack

import concourse.bass as bass
from concourse import mybir

F32 = mybir.dt.float32
F32R = mybir.dt.float32r
BF16 = mybir.dt.bfloat16
U8 = mybir.dt.uint8
ALU = mybir.AluOpType
ACT = mybir.ActivationFunctionType
AX_X = mybir.AxisListType.X
ds = bass.ds

P = 128
EPS = 1e-5
TOP_K = 2
MASKED = -1e30
LOWEST = -1e29


def flamingo_gated_block(nc, x, ctx_t, wqk_t, bqk, gains_bias, attn_mask, key_mask, wg_t, experts, out):
    B, S, D = x.shape
    E = experts.shape[0]
    KC = D // P
    NT = S // P
    PIECES = experts.shape[2]
    FC = PIECES // 3
    GRP = KC * S
    SLOT = PIECES * D
    LAST = B * E - 1
    SCALING = float(P) ** -0.5
    assert (B, S, D, E, FC) == (4, 512, 512, 8, 2)

    with ExitStack() as ctx:
        def sb(name, shape, dt=F32):
            return ctx.enter_context(nc.sbuf_tensor(name, shape, dt))

        def psum(name, shape=(P, 512)):
            return ctx.enter_context(nc.psum_tensor(name, list(shape), F32))

        def sem(name):
            return ctx.enter_context(nc.semaphore(name))

        acc = sb("acc", [P, B * NT * D])
        xt_hi = sb("xt_hi", [P, B * GRP], F32R)
        xt_lo = sb("xt_lo", [P, B * GRP], F32R)
        w_hi = sb("w_hi", [P, 2, PIECES, D], F32R)
        w_lo = sb("w_lo", [P, 2, PIECES, D], F32R)
        w_raw = sb("w_raw", [P, PIECES, D])
        g_hi = sb("g_hi", [P, 2, FC, S], F32R)
        g_lo = sb("g_lo", [P, 2, FC, S], F32R)
        th = sb("th", [P, FC, S])
        gate = sb("gate", [P, FC, S])
        ctx_sb = sb("ctx_sb", [P, S])
        wqk_sb = sb("wqk_sb", [P, 2 * P])
        bqk_sb = sb("bqk_sb", [P, 2])
        q_sb = sb("q_sb", [P, S])
        k_sb = sb("k_sb", [P, S])
        attn_neg = sb("attn_neg", [P, NT, S], BF16)
        key_u8 = sb("key_u8", [P, B * S], U8)
        key_neg = sb("key_neg", [P, S], BF16)
        neg = sb("neg", [P, 2, S], BF16)
        prob = sb("prob", [P, 2, S])
        xn = sb("xn", [P, D])
        xt_f32 = sb("xt_f32", [P, KC, P])
        ident = sb("ident", [P, P])
        attn_u8 = gate[:, 0, :].bitcast(U8).rearrange("p (t s) -> p t s", t=NT)
        bn1 = sb("bn1", [P, NT, 6])
        mv1 = sb("mv1", [P, NT, 2])
        ve1 = sb("ve1", [P, NT])
        rstd1 = sb("rstd1", [P, NT])
        rs1 = sb("rs1", [P, NT])
        zmax = sb("zmax", [P, NT])
        nbias = sb("nbias", [P, NT])
        psum_row = sb("psum_row", [P, NT])
        rden = sb("rden", [P, NT])
        rgain = sb("rgain", [P, NT])
        bn2 = sb("bn2", [P, NT, 6])
        mv2 = sb("mv2", [P, NT, 2])
        ve2 = sb("ve2", [P, NT])
        rstd2 = sb("rstd2", [P, NT])
        minus_half = sb("minus_half", [P, NT])
        gb_sb = sb("gb_sb", [P, 2 + E])
        tg = sb("tg", [P, 2])
        half_gain = sb("half_gain", [P, 1])
        wg_sb = sb("wg_sb", [P, KC, E])
        lg = sb("lg", [P, NT, E])
        lt = sb("lt", [P, NT, E])
        sig = sb("sig", [P, NT, E])
        sc = sb("sc", [P, NT, E])
        before = sb("before", [P, E, E], BF16)
        above = sb("above", [P, NT, E, E], BF16)
        ties = sb("ties", [P, NT, E, E], BF16)
        rank = sb("rank", [P, NT, E])
        picked = sb("picked", [P, NT, E])
        wsum = sb("wsum", [P, NT])
        wrec = sb("wrec", [P, NT])
        wts = sb("wts", [P, B * NT * E])

        ps_h = [[psum(f"ps_h{m}_{c}") for c in range(FC)] for m in (1, 3)]
        ps_o = [psum(f"ps_o{i}") for i in range(2)]
        ps_s = psum("ps_s")
        ps_t = psum("ps_t")

        s_const = sem("s_const")
        s_masks_in = sem("s_masks_in")
        s_ctx_in = sem("s_ctx_in")
        s_x_in = sem("s_x_in")
        s_w_in = sem("s_w_in")
        s_out = sem("s_out")
        s_zero = sem("s_zero")
        s_ident = sem("s_ident")
        s_half = sem("s_half")
        s_attn_neg = sem("s_attn_neg")
        s_key01 = sem("s_key01")
        s_key_neg = sem("s_key_neg")
        s_neg = sem("s_neg")
        s_rstd1 = sem("s_rstd1")
        s_rstd2 = sem("s_rstd2")
        s_xlo = sem("s_xlo")
        s_glo = sem("s_glo")
        s_whi = sem("s_whi")
        s_wlo = sem("s_wlo")
        s_proj = sem("s_proj")
        s_scores = sem("s_scores")
        s_xpose = sem("s_xpose")
        s_logits = sem("s_logits")
        s_h1 = sem("s_h1")
        s_h3 = sem("s_h3")
        s_o = sem("s_o")
        s_tg = sem("s_tg")
        s_qk = sem("s_qk")
        s_exp = sem("s_exp")
        s_xt32 = sem("s_xt32")
        s_xhi = sem("s_xhi")
        s_lt = sem("s_lt")
        s_th = sem("s_th")
        s_ghi = sem("s_ghi")
        s_bn1 = sem("s_bn1")
        s_mv1 = sem("s_mv1")
        s_ve1 = sem("s_ve1")
        s_rs1 = sem("s_rs1")
        s_z = sem("s_z")
        s_zmax = sem("s_zmax")
        s_nb = sem("s_nb")
        s_rden = sem("s_rden")
        s_rgain = sem("s_rgain")
        s_x1 = sem("s_x1")
        s_bn2 = sem("s_bn2")
        s_mv2 = sem("s_mv2")
        s_ve2 = sem("s_ve2")
        s_xn = sem("s_xn")
        s_lg = sem("s_lg")
        s_rt = sem("s_rt")
        s_wts = sem("s_wts")
        s_hg = sem("s_hg")
        s_gate = sem("s_gate")
        s_prod = sem("s_prod")
        s_acc = sem("s_acc")

        s_apart_dve = sem("s_apart_dve")
        s_apart_pool = sem("s_apart_pool")

        RT = 10

        block = ctx.enter_context(nc.Block())

        @block.sync
        def _(sp):
            def load_ctx(b):
                sp.dma_start(ctx_sb[:], ctx_t[ds(b, 1)].rearrange("a p n -> p (a n)")).then_inc(s_ctx_in, 16)

            def load_x(b):
                sp.dma_start(acc[:, ds(b * (NT * D), NT * D)].rearrange("p (t n) -> p t n", t=NT),
                             x[ds(b, 1)].rearrange("a (t p) n -> p (a t) n", p=P)).then_inc(s_x_in, 16)

            def load_expert(e):
                sp.dma_start(w_raw[:], experts[ds(e, 1)].rearrange("a p m n -> p (a m) n")).then_inc(s_w_in, 16)

            sp.dma_start(wqk_sb[:], wqk_t).then_inc(s_const, 16)
            load_ctx(0)
            load_x(0)
            sp.dma_start(bqk_sb[:], bqk).then_inc(s_const, 16)
            sp.dma_start(gb_sb[:], gains_bias.partition_broadcast(P)).then_inc(s_const, 16)
            sp.dma_start(wg_sb[:], wg_t).then_inc(s_const, 16)
            sp.dma_start(attn_u8, attn_mask.rearrange("(t p) n -> p t n", p=P)).then_inc(s_masks_in, 16)
            sp.dma_start(key_u8[:], key_mask.partition_broadcast(P)).then_inc(s_masks_in, 16)
            load_expert(0)
            sp.wait_ge(s_x_in, 16)
            load_x(1)
            sp.wait_ge(s_proj, 2)
            load_ctx(1)
            sp.wait_ge(s_wlo, 2)
            load_expert(1)
            with sp.Fori(2, B) as b:
                sp.wait_ge(s_x_in, 16 * b)
                load_x(b)
                sp.wait_ge(s_proj, 2 * b)
                load_ctx(b)
            with sp.Fori(2, E) as e:
                sp.wait_ge(s_wlo, 2 * e)
                load_expert(e)

            def store_tile(tile, t):
                sp.dma_start(out[ds(tile, 1)].rearrange("a p n -> p (a n)"),
                             acc[:, ds(tile * D, D)]).then_inc(s_out, 16)

            with sp.Fori(0, B) as g:
                for t in range(NT):
                    sp.wait_ge(s_acc, (g + B * (E - 1)) * NT + t + 1)
                    store_tile(g * NT + t, t)
            sp.wait_ge(s_out, 16 * B * NT)

        @block.gpsimd
        def _(pool):
            def wait_apart(done, value):
                pool.wait_ge(done, value)
                if not isinstance(value, int):
                    pool.sem_inc(s_apart_pool, 1)

            def key_mask_row(b):
                if not (isinstance(b, int) and b < 1):
                    wait_apart(s_neg, NT * b)
                pool.tensor_copy(key_neg[:], key_u8[:, ds(b * S, S)]).then_inc(s_key01, 1)
                wait_apart(s_key01, b + 1)
                pool.tensor_scalar(key_neg[:], key_neg[:], MASKED, 1.0, ALU.mult,
                                   ALU.mult).then_inc(s_key_neg, 1)

            def masks(b, t):
                tile = b * NT + t
                pool.wait_ge(s_key_neg, b + 1)
                if not (isinstance(tile, int) and tile < 2):
                    pool.wait_ge(s_zmax, tile - 1)
                pool.tensor_tensor(neg[:, t % 2, :], attn_neg[:, t, :], key_neg[:], ALU.add).then_inc(s_neg, 1)

            def rstd_first(b):
                pool.wait_ge(s_ve1, b + 1)
                pool.tensor_tensor(rstd1[:], ve1[:], minus_half[:], ALU.pow).then_inc(s_rstd1, 1)

            def rstd_second(b, t):
                pool.wait_ge(s_ve2, b * NT + t + 1)
                pool.tensor_tensor(rstd2[:, t:t + 1], ve2[:, t:t + 1], minus_half[:, t:t + 1],
                                   ALU.pow).then_inc(s_rstd2, 1)

            def split_x_lo(b, t):
                tile = b * NT + t
                pool.wait_ge(s_xhi, tile + 1)
                cols = (slice(None), slice(None), slice(t * P, (t + 1) * P))
                hi = xt_hi[:, ds(b * GRP, GRP)].rearrange("p (k s) -> p k s", k=KC)[cols]
                lo = xt_lo[:, ds(b * GRP, GRP)].rearrange("p (k s) -> p k s", k=KC)[cols]
                pool.tensor_tensor(lo, xt_f32[:], hi.bitcast(F32), ALU.subtract).then_inc(s_xlo, 1)

            def split_g_lo(n, par, c):
                pool.wait_ge(s_ghi, n * FC + c + 1)
                pool.tensor_tensor(g_lo[:, par, c, :], gate[:, c, :], g_hi[:, par, c, :].bitcast(F32),
                                   ALU.subtract).then_inc(s_glo, 1)

            def split_w_lo(e, slot, a, z):
                pool.tensor_tensor(w_lo[:, slot, a:z, :], w_raw[:, a:z, :], w_hi[:, slot, a:z, :].bitcast(F32),
                                   ALU.subtract).then_inc(s_wlo, 1)

            def split_w(e, slot, part):
                a, z = ((0, 2 * FC), (2 * FC, 3 * FC))[part]
                pool.tensor_copy(w_hi[:, slot, a:z, :], w_raw[:, a:z, :]).then_inc(s_whi, 1)
                pool.wait_ge(s_whi, 2 * e + part + 1)
                split_w_lo(e, slot, a, z)

            pool.memset(ident[:], 0.0).then_inc(s_zero, 1)
            pool.memset(before[:], 1.0).then_inc(s_zero, 1)
            pool.memset(minus_half[:], -0.5).then_inc(s_half, 1)
            pool.wait_ge(s_zero, 2)
            pool.affine_select(out=ident[:], in_=ident[:], compare_op=ALU.not_equal, fill=1.0, base=0,
                               pattern=[[-1, P]], channel_multiplier=1).then_inc(s_ident, 1)
            pool.affine_select(out=before[:], in_=before[:], compare_op=ALU.is_gt, fill=0.0, base=0,
                               pattern=[[1, E], [-1, E]], channel_multiplier=0).then_inc(s_ident, 1)
            pool.wait_ge(s_half, 1)
            pool.wait_ge(s_masks_in, 32)

            pool.tensor_scalar(attn_neg[:], attn_u8, MASKED, 1.0, ALU.mult, ALU.mult).then_inc(s_attn_neg, 1)
            pool.wait_ge(s_attn_neg, 1)

            key_mask_row(0)
            masks(0, 0)
            masks(0, 1)
            rstd_first(0)
            masks(0, 2)
            rstd_second(0, 0)
            pool.wait_ge(s_whi, 1)
            split_w_lo(0, 0, 0, 2 * FC)
            rstd_second(0, 1)
            masks(0, 3)
            split_x_lo(0, 0)
            rstd_second(0, 2)
            split_x_lo(0, 1)
            rstd_second(0, 3)
            split_x_lo(0, 2)
            pool.wait_ge(s_whi, 2)
            split_w_lo(0, 0, 2 * FC, 3 * FC)
            split_x_lo(0, 3)

            def pair(b):
                key_mask_row(b + 1)
                masks(b + 1, 0)
                rstd_first(b + 1)
                masks(b + 1, 1)
                masks(b + 1, 2)
                split_g_lo(2 * b, 0, 0)
                rstd_second(b + 1, 0)
                masks(b + 1, 3)
                split_g_lo(2 * b, 0, 1)
                rstd_second(b + 1, 1)
                split_x_lo(b + 1, 0)
                if isinstance(b, int) and b == 0:
                    for part, (a, z) in enumerate(((0, 2 * FC), (2 * FC, 3 * FC))):
                        pool.wait_ge(s_whi, 3 + part)
                        split_w_lo(1, 1, a, z)
                rstd_second(b + 1, 2)
                split_x_lo(b + 1, 1)
                split_g_lo(2 * b + 1, 1, 0)
                split_x_lo(b + 1, 2)
                rstd_second(b + 1, 3)
                split_g_lo(2 * b + 1, 1, 1)
                split_x_lo(b + 1, 3)

            pair(0)
            with pool.Fori(1, B - 1) as b:
                pair(b)
            n = 2 * (B - 1)
            split_g_lo(n, 0, 0)
            split_g_lo(n, 0, 1)
            pool.wait_ge(s_w_in, 16 * 3)
            pool.wait_ge(s_h3, FC * (n + 1))
            split_w(2, 0, 0)
            split_g_lo(n + 1, 1, 0)
            split_g_lo(n + 1, 1, 1)
            pool.wait_ge(s_o, NT * (n + 1))
            split_w(2, 0, 1)

            def expert(e, slot, loads_next):
                for g in range(B):
                    n = B * e + g
                    split_g_lo(n, g % 2, 0)
                    split_g_lo(n, g % 2, 1)
                    if loads_next and g in (1, 2):
                        if g == 1:
                            pool.wait_ge(s_w_in, 16 * (e + 2))
                            wait_apart(s_o, NT * B * e)
                        split_w(e + 1, 1 - slot, g - 1)

            with pool.Fori(1, E // 2 - 1) as p:
                for slot in range(2):
                    expert(2 * p + slot, slot, True)
            expert(E - 2, 0, True)
            expert(E - 1, 1, False)

        @block.scalar
        def _(act):
            def project(b, i):
                act.wait_ge(s_proj, 2 * b + i + 1)
                act.activation((q_sb, k_sb)[i][:], ps_s[:], ACT.Identity,
                               bias=bqk_sb[:, i:i + 1]).then_inc(s_qk, 1)

            def exponentials(b, t):
                act.wait_ge(s_nb, b * NT + t + 1)
                act.activation(prob[:, t % 2, :], prob[:, t % 2, :], ACT.Exp, bias=nbias[:, t:t + 1],
                               scale=rs1[:, t:t + 1], accum_out=psum_row[:, t:t + 1]).then_inc(s_exp, 1)

            def transposed(b, t):
                tile = b * NT + t
                act.wait_ge(s_xpose, tile + 1)
                if not (isinstance(tile, int) and tile < 1):
                    act.wait_ge(s_logits, tile)
                    act.wait_ge(s_xlo, tile)
                src = ps_t[:].rearrange("p (k s) -> p k s", k=KC)
                act.copy(xt_f32[:], src).then_inc(s_xt32, 1)
                act.copy(xt_hi[:, ds(b * GRP, GRP)].rearrange("p (k s) -> p k s", k=KC)[:, :, t * P:(t + 1) * P],
                         src).then_inc(s_xhi, 1)

            def router_tanh(b):
                act.wait_ge(s_lg, NT * (b + 1))
                act.activation(lt[:], lg[:], ACT.Tanh, scale=0.5).then_inc(s_lt, 1)

            def hidden_tanh(n, c):
                k = n * FC + c
                act.wait_ge(s_h1, k + 1)
                if not (isinstance(k, int) and k < FC):
                    act.wait_ge(s_gate, k - FC + 1)
                act.activation(th[:, c, :], ps_h[0][c][:], ACT.Tanh, scale=0.5).then_inc(s_th, 1)

            def split_g_hi(n, par, c):
                k = n * FC + c
                act.wait_ge(s_prod, k + 1)
                if not (isinstance(n, int) and n < 2):
                    act.wait_ge(s_o, NT * (n - 1))
                act.copy(g_hi[:, par, c, :], gate[:, c, :]).then_inc(s_ghi, 1)

            def split_w_hi(slot):
                for a, z in ((0, 2 * FC), (2 * FC, 3 * FC)):
                    act.copy(w_hi[:, slot, a:z, :], w_raw[:, a:z, :]).then_inc(s_whi, 1)

            act.wait_ge(s_const, 64)
            act.activation(tg[:], gb_sb[:, 0:2], ACT.Tanh).then_inc(s_tg, 1)
            project(0, 0)
            project(0, 1)
            exponentials(0, 0)
            act.wait_ge(s_w_in, 16)
            split_w_hi(0)
            exponentials(0, 1)
            transposed(0, 0)
            exponentials(0, 2)
            transposed(0, 1)
            exponentials(0, 3)
            transposed(0, 2)
            transposed(0, 3)

            def pair(b):
                router_tanh(b)
                project(b + 1, 0)
                project(b + 1, 1)
                hidden_tanh(2 * b, 0)
                exponentials(b + 1, 0)
                split_g_hi(2 * b, 0, 0)
                hidden_tanh(2 * b, 1)
                if isinstance(b, int) and b == 0:
                    act.wait_ge(s_w_in, 32)
                    split_w_hi(1)
                exponentials(b + 1, 1)
                split_g_hi(2 * b, 0, 1)
                transposed(b + 1, 0)
                exponentials(b + 1, 2)
                transposed(b + 1, 1)
                hidden_tanh(2 * b + 1, 0)
                split_g_hi(2 * b + 1, 1, 0)
                exponentials(b + 1, 3)
                hidden_tanh(2 * b + 1, 1)
                transposed(b + 1, 2)
                split_g_hi(2 * b + 1, 1, 1)
                transposed(b + 1, 3)

            pair(0)
            with act.Fori(1, B - 1) as b:
                pair(b)
            router_tanh(B - 1)

            def hidden(n, par):
                hidden_tanh(n, 0)
                split_g_hi(n, par, 0)
                hidden_tanh(n, 1)
                split_g_hi(n, par, 1)

            with act.Fori(B - 1, B * E // 2) as u:
                hidden(2 * u, 0)
                hidden(2 * u + 1, 1)

        @block.vector
        def _(dve):
            def wait_apart(done, value):
                dve.wait_ge(done, value)
                if not isinstance(value, int):
                    dve.sem_inc(s_apart_dve, 1)

            def first_stats(b):
                wait_apart(s_x_in, 16 * (b + 1))
                for t in range(NT):
                    dve.bn_stats(bn1[:, t, :], acc[:, ds((b * NT + t) * D, D)]).then_inc(s_bn1, 1)
                for t in range(NT):
                    wait_apart(s_bn1, b * NT + t + 1)
                    dve.bn_aggr(mv1[:, t, :], bn1[:, t, :]).then_inc(s_mv1, 1)
                dve.wait_ge(s_mv1, NT * (b + 1))
                dve.tensor_scalar(ve1[:], mv1[:, :, 1], EPS, None, ALU.add).then_inc(s_ve1, 1)

            def first_scale(b):
                dve.wait_ge(s_rstd1, b + 1)
                dve.tensor_scalar(rs1[:], rstd1[:], SCALING, None, ALU.mult).then_inc(s_rs1, 1)

            def scores(b, t):
                tile = b * NT + t
                dve.wait_ge(s_scores, tile + 1)
                dve.scalar_tensor_tensor(out=prob[:, t % 2, :], in0=acc[:, ds(tile * D, D)],
                                         scalar=mv1[:, t, 0:1], in1=ps_s[:], op0=ALU.subtract,
                                         op1=ALU.mult).then_inc(s_z, 1)
                dve.wait_ge(s_z, tile + 1)
                wait_apart(s_neg, tile + 1)
                dve.tensor_tensor_reduce(prob[:, t % 2, :], prob[:, t % 2, :], neg[:, t % 2, :], 1.0, LOWEST,
                                         ALU.add, ALU.max, zmax[:, t:t + 1]).then_inc(s_zmax, 1)
                dve.wait_ge(s_zmax, tile + 1)
                dve.wait_ge(s_rs1, b + 1)
                dve.scalar_tensor_tensor(out=nbias[:, t:t + 1], in0=zmax[:, t:t + 1], scalar=-1.0,
                                         in1=rs1[:, t:t + 1], op0=ALU.mult, op1=ALU.mult).then_inc(s_nb, 1)

            def residual(b, t):
                tile = b * NT + t
                row = acc[:, ds(tile * D, D)]
                dve.wait_ge(s_exp, tile + 1)
                dve.reciprocal(rden[:, t:t + 1], psum_row[:, t:t + 1]).then_inc(s_rden, 1)
                dve.wait_ge(s_rden, tile + 1)
                dve.tensor_scalar(rgain[:, t:t + 1], rden[:, t:t + 1], tg[:, 0:1], None,
                                  ALU.mult).then_inc(s_rgain, 1)
                dve.wait_ge(s_rgain, tile + 1)
                dve.scalar_tensor_tensor(out=row, in0=prob[:, t % 2, :], scalar=rgain[:, t:t + 1], in1=row,
                                         op0=ALU.mult, op1=ALU.add).then_inc(s_x1, 1)
                wait_apart(s_x1, tile + 1)
                dve.bn_stats(bn2[:, t, :], row).then_inc(s_bn2, 1)
                wait_apart(s_bn2, tile + 1)
                dve.bn_aggr(mv2[:, t, :], bn2[:, t, :]).then_inc(s_mv2, 1)
                dve.wait_ge(s_mv2, tile + 1)
                dve.tensor_scalar(ve2[:, t:t + 1], mv2[:, t, 1:2], EPS, None, ALU.add).then_inc(s_ve2, 1)

            def normed(b, t):
                tile = b * NT + t
                dve.wait_ge(s_rstd2, tile + 1)
                if not (isinstance(tile, int) and tile < 1):
                    dve.wait_ge(s_xpose, tile)
                dve.tensor_scalar(xn[:], acc[:, ds(tile * D, D)], mv2[:, t, 0:1], rstd2[:, t:t + 1],
                                  ALU.subtract, ALU.mult).then_inc(s_xn, 1)

            def logits(b, t):
                dve.wait_ge(s_logits, b * NT + t + 1)
                if t == 0 and not (isinstance(b, int) and b < 1):
                    dve.wait_ge(s_lt, b)
                dve.tensor_copy(lg[:, t, :], ps_t[:, 0:E]).then_inc(s_lg, 1)

            def router(b):
                step = [0]

                def done(ins):
                    step[0] += 1
                    ins.then_inc(s_rt, 1)
                    dve.wait_ge(s_rt, b * RT + step[0])

                full = [P, NT, E, E]
                dve.wait_ge(s_lt, b + 1)
                done(dve.tensor_scalar(sig[:], lt[:], 0.5, 0.5, ALU.mult, ALU.add))
                bias = gb_sb[:, 2:2 + E].unsqueeze(1).to_broadcast([P, NT, E])
                done(dve.tensor_tensor(sc[:], sig[:], bias, ALU.add))
                other = sc[:].unsqueeze(2).to_broadcast(full)
                own = sc[:].unsqueeze(3).to_broadcast(full)
                done(dve.tensor_tensor(above[:], other, own, ALU.is_gt))
                done(dve.tensor_tensor(ties[:], other, own, ALU.is_equal))
                done(dve.tensor_tensor(ties[:], ties[:], before[:].unsqueeze(1).to_broadcast(full), ALU.mult))
                done(dve.tensor_tensor(above[:], above[:], ties[:], ALU.add))
                done(dve.tensor_reduce(rank[:], above[:], AX_X, ALU.add))
                done(dve.scalar_tensor_tensor(out=picked[:], in0=rank[:], scalar=float(TOP_K), in1=sig[:],
                                              op0=ALU.is_lt, op1=ALU.mult))
                done(dve.tensor_reduce(wsum[:], picked[:], AX_X, ALU.add))
                done(dve.reciprocal(wrec[:], wsum[:]))
                dve.scalar_tensor_tensor(out=wts[:, ds(b * (NT * E), NT * E)].rearrange("p (t e) -> p t e", t=NT),
                                         in0=picked[:], scalar=half_gain[:],
                                         in1=wrec[:].unsqueeze(2).to_broadcast([P, NT, E]),
                                         op0=ALU.mult, op1=ALU.mult).then_inc(s_wts, 1)

            def gated(n, c):
                k = n * FC + c
                dve.wait_ge(s_th, k + 1)
                if not (isinstance(k, int) and k < FC):
                    dve.wait_ge(s_glo, k - FC + 1)
                dve.scalar_tensor_tensor(out=gate[:, c, :], in0=th[:, c, :], scalar=1.0, in1=ps_h[0][c][:],
                                         op0=ALU.add, op1=ALU.mult).then_inc(s_gate, 1)

            def times_h3(n, c):
                k = n * FC + c
                dve.wait_ge(s_h3, k + 1)
                dve.wait_ge(s_gate, k + 1)
                dve.tensor_tensor(gate[:, c, :], gate[:, c, :], ps_h[1][c][:], ALU.mult).then_inc(s_prod, 1)

            def add_output(n, e, g, t):
                dve.wait_ge(s_o, n * NT + t + 1)
                row = acc[:, ds((g * NT + t) * D, D)]
                dve.scalar_tensor_tensor(out=row, in0=ps_o[t % 2][:],
                                         scalar=wts[:, ds((g * NT + t) * E + e, 1)], in1=row,
                                         op0=ALU.mult, op1=ALU.add).then_inc(s_acc, 1)

            dve.wait_ge(s_tg, 1)
            dve.tensor_scalar(half_gain[:], tg[:, 1:2], 0.5, None, ALU.mult).then_inc(s_hg, 1)
            first_stats(0)
            first_scale(0)
            scores(0, 0)
            scores(0, 1)
            residual(0, 0)
            normed(0, 0)
            scores(0, 2)
            residual(0, 1)
            normed(0, 1)
            logits(0, 0)
            scores(0, 3)
            residual(0, 2)
            normed(0, 2)
            logits(0, 1)
            residual(0, 3)
            normed(0, 3)
            logits(0, 2)
            logits(0, 3)
            dve.wait_ge(s_hg, 1)
            dve.wait_ge(s_ident, 2)

            def pair(b):
                first = isinstance(b, int) and b == 0
                n = 2 * b
                first_stats(b + 1)
                router(b)
                gated(n, 0)
                first_scale(b + 1)
                scores(b + 1, 0)
                times_h3(n, 0)
                gated(n, 1)
                residual(b + 1, 0)
                normed(b + 1, 0)
                scores(b + 1, 1)
                times_h3(n, 1)
                if not first:
                    dve.wait_ge(s_wts, b)
                    add_output(n - 1, 1, b - 1, 0)
                residual(b + 1, 1)
                if not first:
                    add_output(n - 1, 1, b - 1, 1)
                normed(b + 1, 1)
                if not first:
                    add_output(n - 1, 1, b - 1, 2)
                logits(b + 1, 0)
                scores(b + 1, 2)
                if not first:
                    add_output(n - 1, 1, b - 1, 3)
                residual(b + 1, 2)
                gated(n + 1, 0)
                normed(b + 1, 2)
                times_h3(n + 1, 0)
                logits(b + 1, 1)
                scores(b + 1, 3)
                gated(n + 1, 1)
                residual(b + 1, 3)
                times_h3(n + 1, 1)
                logits(b + 1, 2)
                normed(b + 1, 3)
                dve.wait_ge(s_wts, b + 1)
                for t in range(NT):
                    add_output(n, 0, b, t)
                logits(b + 1, 3)

            pair(0)
            with dve.Fori(1, B - 1) as b:
                pair(b)
            router(B - 1)
            dve.wait_ge(s_wts, B)

            def unit(n, prev_n, prev_e, prev_g):
                for c in range(FC):
                    gated(n, c)
                    times_h3(n, c)
                for t in range(NT):
                    add_output(prev_n, prev_e, prev_g, t)

            unit(2 * B - 2, 2 * B - 3, 1, B - 2)
            unit(2 * B - 1, 2 * B - 2, 0, B - 1)
            unit(2 * B, 2 * B - 1, 1, B - 1)
            unit(2 * B + 1, 2 * B, 2, 0)
            unit(2 * B + 2, 2 * B + 1, 2, 1)
            unit(2 * B + 3, 2 * B + 2, 2, 2)
            with dve.Fori(3, E) as e:
                unit(B * e, B * e - 1, e - 1, B - 1)
                with dve.Fori(1, B) as g:
                    unit(B * e + g, B * e + g - 1, e, g - 1)
            for t in range(NT):
                add_output(LAST, E - 1, B - 1, t)

        @block.tensor
        def _(pe):
            def project(b, i):
                pe.wait_ge(s_ctx_in, 16 * (b + 1))
                if i == 1:
                    pe.wait_ge(s_qk, 2 * b + 1)
                elif not (isinstance(b, int) and b == 0):
                    pe.wait_ge(s_z, NT * b)
                pe.matmul(ps_s[:], wqk_sb[:, i * P:(i + 1) * P], ctx_sb[:], start=True,
                          stop=True).then_inc(s_proj, 1)

            def scores(b, t):
                pe.wait_ge(s_qk, 2 * b + 2)
                if t > 0:
                    pe.wait_ge(s_z, b * NT + t)
                pe.matmul(ps_s[:], q_sb[:, t * P:(t + 1) * P], k_sb[:], start=True,
                          stop=True).then_inc(s_scores, 1)

            def transpose(b, t):
                tile = b * NT + t
                pe.wait_ge(s_xn, tile + 1)
                if not (isinstance(tile, int) and tile < 1):
                    pe.wait_ge(s_lg, tile)
                for k in range(KC):
                    mm = pe.transpose(ps_t[:, k * P:(k + 1) * P], xn[:, k * P:(k + 1) * P], ident[:])
                mm.then_inc(s_xpose, 1)

            def logits(b, t):
                pe.wait_ge(s_xt32, b * NT + t + 1)
                pe.wait_ge(s_xhi, b * NT + t + 1)
                for k in range(KC):
                    mm = pe.matmul(ps_t[:, 0:E], xt_f32[:, k, :], wg_sb[:, k, :], start=(k == 0),
                                   stop=(k == KC - 1))
                mm.then_inc(s_logits, 1)

            def hidden(n, slot, g, c, m):
                kk = n * FC + c
                if not (isinstance(n, int) and n == 0):
                    pe.wait_ge((s_gate, s_prod)[m], kk - FC + 1)
                bank = ps_h[m][c]
                for k in range(KC):
                    w = slice(k * P, (k + 1) * P)
                    hi = w_hi[:, slot, 2 * c + m, w]
                    lo = w_lo[:, slot, 2 * c + m, w]
                    x_hi = xt_hi[:, ds(g * GRP + k * S, S)]
                    x_lo = xt_lo[:, ds(g * GRP + k * S, S)]
                    pe.matmul(bank[:], hi, x_hi, start=(k == 0), stop=False)
                    pe.matmul(bank[:], hi, x_lo, start=False, stop=False)
                    mm = pe.matmul(bank[:], lo, x_hi, start=False, stop=(k == KC - 1))
                mm.then_inc((s_h1, s_h3)[m], 1)

            def output(n, par, slot, t):
                if t == 0:
                    pe.wait_ge(s_ghi, FC * (n + 1))
                    pe.wait_ge(s_glo, FC * (n + 1))
                if not (isinstance(n, int) and n == 0 and t < 2):
                    pe.wait_ge(s_acc, n * NT + t - 1)
                bank = ps_o[t % 2]
                tok = slice(t * P, (t + 1) * P)
                for c in range(FC):
                    pe.matmul(bank[:], g_hi[:, par, c, tok], w_hi[:, slot, 2 * FC + c, :],
                              start=(c == 0), stop=False)
                    pe.matmul(bank[:], g_hi[:, par, c, tok], w_lo[:, slot, 2 * FC + c, :],
                              start=False, stop=False)
                    mm = pe.matmul(bank[:], g_lo[:, par, c, tok], w_hi[:, slot, 2 * FC + c, :],
                                   start=False, stop=(c == FC - 1))
                mm.then_inc(s_o, 1)

            pe.wait_ge(s_const, 64)
            pe.wait_ge(s_ident, 2)
            project(0, 0)
            project(0, 1)
            scores(0, 0)
            scores(0, 1)
            transpose(0, 0)
            logits(0, 0)
            scores(0, 2)
            transpose(0, 1)
            logits(0, 1)
            scores(0, 3)
            transpose(0, 2)
            logits(0, 2)
            transpose(0, 3)
            logits(0, 3)

            def pair(b):
                first = isinstance(b, int) and b == 0
                n = 2 * b
                pe.wait_ge(s_xhi, NT * (b + 1))
                pe.wait_ge(s_xlo, NT * (b + 1))
                if first:
                    pe.wait_ge(s_wlo, 1)
                project(b + 1, 0)
                hidden(n, 0, b, 0, 0)
                project(b + 1, 1)
                hidden(n, 0, b, 0, 1)
                scores(b + 1, 0)
                hidden(n, 0, b, 1, 0)
                scores(b + 1, 1)
                hidden(n, 0, b, 1, 1)
                if not first:
                    output(n - 1, 1, 1, 0)
                transpose(b + 1, 0)
                if not first:
                    output(n - 1, 1, 1, 1)
                if not first:
                    output(n - 1, 1, 1, 2)
                logits(b + 1, 0)
                scores(b + 1, 2)
                if not first:
                    output(n - 1, 1, 1, 3)
                transpose(b + 1, 1)
                if first:
                    pe.wait_ge(s_wlo, 3)
                hidden(n + 1, 1, b, 0, 0)
                logits(b + 1, 1)
                scores(b + 1, 3)
                hidden(n + 1, 1, b, 0, 1)
                transpose(b + 1, 2)
                hidden(n + 1, 1, b, 1, 0)
                logits(b + 1, 2)
                hidden(n + 1, 1, b, 1, 1)
                if first:
                    pe.wait_ge(s_wlo, 2)
                output(n, 0, 0, 0)
                transpose(b + 1, 3)
                output(n, 0, 0, 1)
                output(n, 0, 0, 2)
                logits(b + 1, 3)
                output(n, 0, 0, 3)

            pair(0)
            pe.wait_ge(s_wlo, 4)
            with pe.Fori(1, B - 1) as b:
                pair(b)
            pe.wait_ge(s_xhi, NT * B)
            pe.wait_ge(s_xlo, NT * B)

            def unit(n, slot, g, prev_n, prev_par, prev_slot):
                for c in range(FC):
                    hidden(n, slot, g, c, 0)
                    hidden(n, slot, g, c, 1)
                for t in range(NT):
                    output(prev_n, prev_par, prev_slot, t)

            unit(2 * B - 2, 0, B - 1, 2 * B - 3, 1, 1)
            unit(2 * B - 1, 1, B - 1, 2 * B - 2, 0, 0)
            with pe.Fori(1, E // 2) as p:
                for slot in range(2):
                    n = p * (2 * B) + slot * B
                    pe.wait_ge(s_wlo, p * 4 + (2 * slot + 1))
                    unit(n, slot, 0, n - 1, 1, 1 - slot)
                    pe.wait_ge(s_wlo, p * 4 + (2 * slot + 2))
                    unit(n + 1, slot, 1, n, 0, slot)
                    unit(n + 2, slot, 2, n + 1, 1, slot)
                    unit(n + 3, slot, 3, n + 2, 0, slot)
            for t in range(NT):
                output(LAST, 1, 1, t)


def kernel(x, ctx_512, mask_SxS2_bk1, mask_BxS2_bf0, g_xattn, g_ffn, L0_xattn_Wq, L0_xattn_bq, L0_xattn_Wk,
           L0_xattn_bk, L0_ffn_Wg, L0_ffn_W1, L0_ffn_W2, L0_ffn_W3, L0_ffn_bias):
    import numpy as np
    import concourse.bacc as bacc
    from concourse.bass_utils import run_bass_kernel_spmd

    x = np.asarray(x)
    B, S, D = x.shape
    E, F, _ = L0_ffn_W1.shape
    fc, kc = F // P, D // P

    def hidden_layout(w):
        w = np.asarray(w).reshape(E, fc, P, kc, P).transpose(0, 4, 1, 3, 2)
        return w.reshape(E, P, fc, 1, D)

    w13 = np.concatenate([hidden_layout(L0_ffn_W1), hidden_layout(L0_ffn_W3)], axis=3).reshape(E, P, 2 * fc, D)
    w2 = np.asarray(L0_ffn_W2).reshape(E, D, fc, P).transpose(0, 3, 2, 1)
    arrays = {
        "x": x,
        "ctx_t": np.asarray(ctx_512).transpose(0, 2, 1),
        "wqk_t": np.concatenate([np.asarray(L0_xattn_Wq).T, np.asarray(L0_xattn_Wk).T], axis=1),
        "bqk": np.stack([np.asarray(L0_xattn_bq), np.asarray(L0_xattn_bk)], axis=1),
        "gains_bias": np.concatenate([np.asarray(g_xattn), np.asarray(g_ffn), np.asarray(L0_ffn_bias)]),
        "attn_mask": np.asarray(mask_SxS2_bk1),
        "key_mask": np.asarray(mask_BxS2_bf0).reshape(-1),
        "wg_t": np.asarray(L0_ffn_Wg).reshape(E, kc, P).transpose(2, 1, 0),
        "experts": np.concatenate([w13, w2], axis=2),
    }
    arrays = {f"in_{n}": np.ascontiguousarray(a) for n, a in arrays.items()}
    nc = bacc.Bacc("TRN2", target_bir_lowering=False, num_devices=1)
    ins = [nc.dram_tensor(n, a.shape, mybir.dt.from_np(a.dtype), kind="ExternalInput").ap()
           for n, a in arrays.items()]
    out = nc.dram_tensor("out", (B * S // P, P, D), F32, kind="ExternalOutput").ap()
    flamingo_gated_block(nc, *ins, out)
    r = run_bass_kernel_spmd(nc, [arrays], core_ids=[0])
    return r.results[0]["out"].reshape(B, S, D)
```

```python
from contextlib import ExitStack

import concourse.bass as bass
from concourse import mybir

F32 = mybir.dt.float32
F32R = mybir.dt.float32r
BF16 = mybir.dt.bfloat16
U8 = mybir.dt.uint8
ALU = mybir.AluOpType
ACT = mybir.ActivationFunctionType
AX_X = mybir.AxisListType.X
ds = bass.ds

P = 128
EPS = 1e-5
TOP_K = 2
MASKED = -1e30
LOWEST = -1e29


def flamingo_gated_block(nc, x, ctx_t, wqk_t, bqk, gains_bias, attn_mask, key_mask, wg_t, experts, out):
    B, S, D = x.shape
    E = experts.shape[0]
    KC = D // P
    NT = S // P
    PIECES = experts.shape[2]
    FC = PIECES // 3
    PARTS = 3
    GRP = KC * S
    SLOT = PIECES * D
    LAST = B * E - 1
    SCALING = float(P) ** -0.5
    assert (B, S, D, E, FC) == (4, 512, 512, 8, 2)

    with ExitStack() as ctx:
        def sb(name, shape, dt=F32):
            return ctx.enter_context(nc.sbuf_tensor(name, shape, dt))

        def psum(name, shape=(P, 512)):
            return ctx.enter_context(nc.psum_tensor(name, list(shape), F32))

        def sem(name):
            return ctx.enter_context(nc.semaphore(name))

        acc = sb("acc", [P, B * NT * D])
        xt_hi = sb("xt_hi", [P, B * GRP], F32R)
        xt_lo = sb("xt_lo", [P, B * GRP], F32R)
        w_hi = sb("w_hi", [P, 2, PIECES, D], F32R)
        w_lo = sb("w_lo", [P, 2, PIECES, D], F32R)
        w_raw = sb("w_raw", [P, PIECES, D])
        g_hi = sb("g_hi", [P, 2, FC, S], F32R)
        g_lo = sb("g_lo", [P, 2, FC, S], F32R)
        th = sb("th", [P, FC, S])
        gate = sb("gate", [P, FC, S])
        ctx_sb = sb("ctx_sb", [P, S])
        wqk_sb = sb("wqk_sb", [P, 2 * P])
        bqk_sb = sb("bqk_sb", [P, 2])
        q_sb = sb("q_sb", [P, S])
        k_sb = sb("k_sb", [P, S])
        attn_neg = sb("attn_neg", [P, NT, S], BF16)
        key_u8 = sb("key_u8", [P, B * S], U8)
        key_neg = sb("key_neg", [P, S], BF16)
        neg = sb("neg", [P, 2, S], BF16)
        prob = sb("prob", [P, 2, S])
        xn = sb("xn", [P, D])
        xt_f32 = sb("xt_f32", [P, KC, P])
        ident = sb("ident", [P, P])
        attn_u8 = gate[:, 0, :].bitcast(U8).rearrange("p (t s) -> p t s", t=NT)
        bn1 = sb("bn1", [P, NT, 6])
        mv1 = sb("mv1", [P, NT, 2])
        ve1 = sb("ve1", [P, NT])
        rstd1 = sb("rstd1", [P, NT])
        rs1 = sb("rs1", [P, NT])
        zmax = sb("zmax", [P, NT])
        nbias = sb("nbias", [P, NT])
        psum_row = sb("psum_row", [P, NT])
        rden = sb("rden", [P, NT])
        rgain = sb("rgain", [P, NT])
        sum2 = sb("sum2", [P, NT])
        nmean2 = sb("nmean2", [P, NT])
        sqsum2 = sb("sqsum2", [P, NT])
        ve2 = sb("ve2", [P, NT])
        shift2 = sb("shift2", [P, NT])
        rstd2 = sb("rstd2", [P, NT])
        minus_half = sb("minus_half", [P, NT])
        gb_sb = sb("gb_sb", [P, 2 + E])
        tg = sb("tg", [P, 2])
        half_gain = sb("half_gain", [P, 1])
        wg_sb = sb("wg_sb", [P, KC, E])
        lg = sb("lg", [P, NT, E])
        lt = sb("lt", [P, NT, E])
        sig = sb("sig", [P, NT, E])
        sc = sb("sc", [P, NT, E])
        before = sb("before", [P, E, E], BF16)
        above = sb("above", [P, NT, E, E], BF16)
        ties = sb("ties", [P, NT, E, E], BF16)
        rank = sb("rank", [P, NT, E])
        picked = sb("picked", [P, NT, E])
        wsum = sb("wsum", [P, NT])
        wrec = sb("wrec", [P, NT])
        wts = sb("wts", [P, B * NT * E])

        ps_h = [[psum(f"ps_h{m}_{c}") for c in range(FC)] for m in (1, 3)]
        ps_o = [psum(f"ps_o{i}") for i in range(2)]
        ps_s = psum("ps_s")
        ps_t = psum("ps_t")
        first_s = [ps_o[1], ps_s, ps_o[0], ps_o[1]]
        first_t = [ps_t, ps_s, ps_o[0], ps_o[1]]

        s_wqk_in = sem("s_wqk_in")
        s_const = sem("s_const")
        s_wg_in = sem("s_wg_in")
        s_x0_in = [sem(f"s_x0_in{t}") for t in range(NT)]
        s_masks_in = sem("s_masks_in")
        s_ctx_in = sem("s_ctx_in")
        s_x_in = sem("s_x_in")
        s_w_in = [sem(f"s_w_in{part}") for part in range(PARTS)]
        s_out = sem("s_out")
        s_zero = sem("s_zero")
        s_ident = sem("s_ident")
        s_half = sem("s_half")
        s_attn_neg = sem("s_attn_neg")
        s_neg = sem("s_neg")
        s_rstd1 = sem("s_rstd1")
        s_ve2 = sem("s_ve2")
        s_rstd2 = sem("s_rstd2")
        s_shift2 = sem("s_shift2")
        s_xlo = sem("s_xlo")
        s_glo = sem("s_glo")
        s_whi = sem("s_whi")
        s_wlo = sem("s_wlo")
        s_proj = sem("s_proj")
        s_scores = sem("s_scores")
        s_xpose = sem("s_xpose")
        s_logits = sem("s_logits")
        s_h1 = sem("s_h1")
        s_h3 = sem("s_h3")
        s_o = sem("s_o")
        s_tg = sem("s_tg")
        s_qk = sem("s_qk")
        s_exp = sem("s_exp")
        s_sq = sem("s_sq")
        s_xn = sem("s_xn")
        s_xt32 = sem("s_xt32")
        s_xhi = sem("s_xhi")
        s_lt = sem("s_lt")
        s_th = sem("s_th")
        s_ghi = sem("s_ghi")
        s_bn1 = sem("s_bn1")
        s_mv1 = sem("s_mv1")
        s_ve1 = sem("s_ve1")
        s_rs1 = sem("s_rs1")
        s_z = sem("s_z")
        s_zmax = sem("s_zmax")
        s_nb = sem("s_nb")
        s_rden = sem("s_rden")
        s_rgain = sem("s_rgain")
        s_x1 = sem("s_x1")
        s_nmean = sem("s_nmean")
        s_key_neg = sem("s_key_neg")
        s_lg = sem("s_lg")
        s_rt = sem("s_rt")
        s_wts = sem("s_wts")
        s_hg = sem("s_hg")
        s_wlo0 = sem("s_wlo0")
        s_gate = sem("s_gate")
        s_prod = sem("s_prod")
        s_acc = sem("s_acc")

        s_apart_dve = sem("s_apart_dve")
        s_apart_pool = sem("s_apart_pool")
        s_apart_act = sem("s_apart_act")

        def wlo_count(e, part):
            return 3 * e + (part - 1)

        RT = 10

        block = ctx.enter_context(nc.Block())

        @block.sync
        def _(sp):
            def load_ctx(b):
                sp.dma_start(ctx_sb[:], ctx_t[ds(b, 1)].rearrange("a p n -> p (a n)")).then_inc(s_ctx_in, 16)

            def load_x(b):
                sp.dma_start(acc[:, ds(b * (NT * D), NT * D)].rearrange("p (t n) -> p t n", t=NT),
                             x[ds(b, 1)].rearrange("a (t p) n -> p (a t) n", p=P)).then_inc(s_x_in, 16)

            def load_w(e, part):
                a, z = 2 * part, 2 * part + 2
                sp.dma_start(w_raw[:, a:z, :], experts[ds(e, 1), :, a:z, :].rearrange("a p m n -> p (a m) n")).then_inc(
                    s_w_in[part], 16)

            sp.dma_start(wqk_sb[:], wqk_t).then_inc(s_wqk_in, 16)
            load_ctx(0)
            sp.dma_start(bqk_sb[:], bqk).then_inc(s_const, 16)
            sp.dma_start(gb_sb[:], gains_bias.partition_broadcast(P)).then_inc(s_const, 16)
            for t in range(NT):
                sp.dma_start(acc[:, t * D:(t + 1) * D], x[0, t * P:(t + 1) * P, :]).then_inc(s_x0_in[t], 16)
                if t == 0:
                    sp.dma_start(key_u8[:], key_mask.partition_broadcast(P)).then_inc(s_masks_in, 16)
                    sp.dma_start(attn_u8, attn_mask.rearrange("(t p) n -> p t n", p=P)).then_inc(s_masks_in, 16)
            load_w(0, 0)
            load_w(0, 1)
            sp.dma_start(wg_sb[:], wg_t).then_inc(s_wg_in, 16)
            load_w(0, 2)
            load_x(1)
            sp.wait_ge(s_proj, 2)
            load_ctx(1)
            for part in range(PARTS):
                if part < 2:
                    sp.wait_ge(s_wlo0, part + 1)
                else:
                    sp.wait_ge(s_wlo, wlo_count(0, part))
                load_w(1, part)
            with sp.Fori(2, B) as b:
                sp.wait_ge(s_x_in, 16 * b - 16)
                load_x(b)
                sp.wait_ge(s_proj, 2 * b)
                load_ctx(b)
            with sp.Fori(2, E) as e:
                for part in range(PARTS):
                    sp.wait_ge(s_wlo, wlo_count(e - 1, part))
                    load_w(e, part)

            def store_tile(tile, t):
                sp.dma_start(out[ds(tile, 1)].rearrange("a p n -> p (a n)"),
                             acc[:, ds(tile * D, D)]).then_inc(s_out, 16)

            with sp.Fori(0, B) as g:
                for t in range(NT):
                    sp.wait_ge(s_acc, (g + B * (E - 1)) * NT + t + 1)
                    store_tile(g * NT + t, t)
            sp.wait_ge(s_out, 16 * B * NT)

        @block.gpsimd
        def _(pool):
            def wait_apart(done, value):
                pool.wait_ge(done, value)
                if not isinstance(value, int):
                    pool.sem_inc(s_apart_pool, 1)

            def masks(b, t):
                tile = b * NT + t
                pool.wait_ge(s_key_neg, b + 1)
                if not (isinstance(tile, int) and tile < 2):
                    pool.wait_ge(s_zmax, tile - 1)
                pool.tensor_tensor(neg[:, t % 2, :], attn_neg[:, t, :], key_neg[:], ALU.add).then_inc(s_neg, 1)

            def rstd_first(b):
                pool.wait_ge(s_ve1, b + 1)
                pool.tensor_tensor(rstd1[:], ve1[:], minus_half[:], ALU.pow).then_inc(s_rstd1, 1)

            def rstd_second(b, t):
                tile = b * NT + t
                col = slice(t, t + 1)
                wait_apart(s_sq, tile + 1)
                pool.tensor_scalar(ve2[:, col], sqsum2[:, col], 1.0 / D, EPS, ALU.mult, ALU.add).then_inc(s_ve2, 1)
                pool.wait_ge(s_ve2, tile + 1)
                pool.tensor_tensor(rstd2[:, col], ve2[:, col], minus_half[:, col], ALU.pow).then_inc(s_rstd2, 1)
                pool.wait_ge(s_rstd2, tile + 1)
                pool.tensor_tensor(shift2[:, col], rstd2[:, col], nmean2[:, col], ALU.mult).then_inc(s_shift2, 1)

            def split_x_lo(b, t):
                tile = b * NT + t
                pool.wait_ge(s_xhi, tile + 1)
                cols = (slice(None), slice(None), slice(t * P, (t + 1) * P))
                hi = xt_hi[:, ds(b * GRP, GRP)].rearrange("p (k s) -> p k s", k=KC)[cols]
                lo = xt_lo[:, ds(b * GRP, GRP)].rearrange("p (k s) -> p k s", k=KC)[cols]
                pool.tensor_tensor(lo, xt_f32[:], hi.bitcast(F32), ALU.subtract).then_inc(s_xlo, 1)

            def split_g_lo(n, par, c):
                pool.wait_ge(s_ghi, n * FC + c + 1)
                pool.tensor_tensor(g_lo[:, par, c, :], gate[:, c, :], g_hi[:, par, c, :].bitcast(F32),
                                   ALU.subtract).then_inc(s_glo, 1)

            def split_w_lo(e, slot, part):
                a, z = 2 * part, 2 * part + 2
                pool.wait_ge(s_whi, PARTS * e + part + 1)
                pool.tensor_tensor(w_lo[:, slot, a:z, :], w_raw[:, a:z, :], w_hi[:, slot, a:z, :].bitcast(F32),
                                   ALU.subtract).then_inc(s_wlo, 1)

            def split_w(e, slot, part):
                a, z = 2 * part, 2 * part + 2
                wait_apart(s_w_in[part], 16 * (e + 1))
                pool.tensor_copy(w_hi[:, slot, a:z, :], w_raw[:, a:z, :]).then_inc(s_whi, 1)
                split_w_lo(e, slot, part)

            pool.memset(ident[:], 0.0).then_inc(s_zero, 1)
            pool.memset(before[:], 1.0).then_inc(s_zero, 1)
            pool.memset(minus_half[:], -0.5).then_inc(s_half, 1)
            pool.wait_ge(s_zero, 2)
            pool.affine_select(out=ident[:], in_=ident[:], compare_op=ALU.not_equal, fill=1.0, base=0,
                               pattern=[[-1, P]], channel_multiplier=1).then_inc(s_ident, 1)
            pool.affine_select(out=before[:], in_=before[:], compare_op=ALU.is_gt, fill=0.0, base=0,
                               pattern=[[1, E], [-1, E]], channel_multiplier=0).then_inc(s_ident, 1)
            pool.wait_ge(s_half, 1)
            pool.wait_ge(s_masks_in, 32)

            pool.tensor_scalar(attn_neg[:], attn_u8, MASKED, 1.0, ALU.mult, ALU.mult).then_inc(s_attn_neg, 1)
            pool.wait_ge(s_attn_neg, 1)

            masks(0, 0)
            rstd_first(0)
            masks(0, 1)
            masks(0, 2)
            rstd_second(0, 0)
            masks(0, 3)
            rstd_second(0, 1)
            split_x_lo(0, 0)
            rstd_second(0, 2)
            split_x_lo(0, 1)
            rstd_second(0, 3)
            split_x_lo(0, 2)
            split_x_lo(0, 3)

            masks(1, 0)
            rstd_first(1)
            masks(1, 1)
            split_w_lo(0, 0, 2)
            masks(1, 2)
            rstd_second(1, 0)
            split_w_lo(1, 1, 0)
            rstd_second(1, 1)
            split_w_lo(1, 1, 1)
            split_g_lo(0, 0, 0)
            masks(1, 3)
            split_g_lo(0, 0, 1)
            rstd_second(1, 2)
            split_x_lo(1, 0)
            split_w_lo(1, 1, 2)
            split_x_lo(1, 1)
            split_g_lo(1, 1, 0)
            rstd_second(1, 3)
            split_g_lo(1, 1, 1)
            split_x_lo(1, 2)
            split_x_lo(1, 3)

            def pair(b):
                masks(b + 1, 0)
                rstd_first(b + 1)
                masks(b + 1, 1)
                masks(b + 1, 2)
                rstd_second(b + 1, 0)
                split_g_lo(2 * b, 0, 0)
                masks(b + 1, 3)
                rstd_second(b + 1, 1)
                split_g_lo(2 * b, 0, 1)
                split_x_lo(b + 1, 0)
                split_x_lo(b + 1, 1)
                rstd_second(b + 1, 2)
                split_g_lo(2 * b + 1, 1, 0)
                split_x_lo(b + 1, 2)
                rstd_second(b + 1, 3)
                split_g_lo(2 * b + 1, 1, 1)
                split_x_lo(b + 1, 3)

            with pool.Fori(1, B - 1) as b:
                pair(b)
            n = 2 * (B - 1)
            split_g_lo(n, 0, 0)
            split_g_lo(n, 0, 1)
            pool.wait_ge(s_h3, FC * (n + 1))
            split_w(2, 0, 0)
            split_g_lo(n + 1, 1, 0)
            split_w(2, 0, 1)
            split_g_lo(n + 1, 1, 1)
            pool.wait_ge(s_o, NT * (n + 1))
            split_w(2, 0, 2)

            def expert(e, slot, loads_next):
                for g in range(B):
                    n = B * e + g
                    if loads_next and g > 0:
                        if g == 1:
                            wait_apart(s_o, NT * B * e)
                        split_w(e + 1, 1 - slot, g - 1)
                    split_g_lo(n, g % 2, 0)
                    split_g_lo(n, g % 2, 1)

            with pool.Fori(1, E // 2 - 1) as p:
                for slot in range(2):
                    expert(2 * p + slot, slot, True)
            expert(E - 2, 0, True)
            expert(E - 1, 1, False)

        @block.scalar
        def _(act):
            def wait_apart(done, value):
                act.wait_ge(done, value)
                if not isinstance(value, int):
                    act.sem_inc(s_apart_act, 1)

            def project(b, i, bank=ps_s):
                act.wait_ge(s_proj, 2 * b + i + 1)
                act.activation((q_sb, k_sb)[i][:], bank[:], ACT.Identity,
                               bias=bqk_sb[:, i:i + 1]).then_inc(s_qk, 1)

            def exponentials(b, t):
                act.wait_ge(s_nb, b * NT + t + 1)
                act.activation(prob[:, t % 2, :], prob[:, t % 2, :], ACT.Exp, bias=nbias[:, t:t + 1],
                               scale=rs1[:, t:t + 1], accum_out=psum_row[:, t:t + 1]).then_inc(s_exp, 1)

            def squares(b, t):
                tile = b * NT + t
                wait_apart(s_nmean, tile + 1)
                act.activation(prob[:, t % 2, :], acc[:, ds(tile * D, D)], ACT.Square,
                               bias=nmean2[:, t:t + 1], accum_out=sqsum2[:, t:t + 1]).then_inc(s_sq, 1)

            def normed(b, t):
                tile = b * NT + t
                if not (isinstance(tile, int) and tile < 1):
                    act.wait_ge(s_xpose, tile)
                wait_apart(s_shift2, tile + 1)
                act.activation(xn[:], acc[:, ds(tile * D, D)], ACT.Identity, bias=shift2[:, t:t + 1],
                               scale=rstd2[:, t:t + 1]).then_inc(s_xn, 1)

            def transposed(b, t, bank=ps_t):
                tile = b * NT + t
                act.wait_ge(s_xpose, tile + 1)
                if not (isinstance(tile, int) and tile < 1):
                    act.wait_ge(s_logits, tile)
                    act.wait_ge(s_xlo, tile)
                src = bank[:].rearrange("p (k s) -> p k s", k=KC)
                act.copy(xt_f32[:], src).then_inc(s_xt32, 1)
                act.copy(xt_hi[:, ds(b * GRP, GRP)].rearrange("p (k s) -> p k s", k=KC)[:, :, t * P:(t + 1) * P],
                         src).then_inc(s_xhi, 1)

            def router_tanh(b):
                act.wait_ge(s_lg, NT * (b + 1))
                act.activation(lt[:], lg[:], ACT.Tanh, scale=0.5).then_inc(s_lt, 1)

            def hidden_tanh(n, c):
                k = n * FC + c
                act.wait_ge(s_h1, k + 1)
                if not (isinstance(k, int) and k < FC):
                    act.wait_ge(s_gate, k - FC + 1)
                act.activation(th[:, c, :], ps_h[0][c][:], ACT.Tanh, scale=0.5).then_inc(s_th, 1)

            def split_g_hi(n, par, c):
                k = n * FC + c
                act.wait_ge(s_prod, k + 1)
                if not (isinstance(n, int) and n < 2):
                    act.wait_ge(s_o, NT * (n - 1))
                act.copy(g_hi[:, par, c, :], gate[:, c, :]).then_inc(s_ghi, 1)

            def split_w_hi(slot, part):
                a, z = 2 * part, 2 * part + 2
                act.wait_ge(s_w_in[part], 16 * (slot + 1))
                act.copy(w_hi[:, slot, a:z, :], w_raw[:, a:z, :]).then_inc(s_whi, 1)

            act.wait_ge(s_const, 32)
            act.activation(tg[:], gb_sb[:, 0:2], ACT.Tanh).then_inc(s_tg, 1)
            project(0, 0)
            project(0, 1, ps_o[0])
            exponentials(0, 0)
            split_w_hi(0, 0)
            exponentials(0, 1)
            squares(0, 0)
            split_w_hi(0, 1)
            normed(0, 0)
            exponentials(0, 2)
            squares(0, 1)
            transposed(0, 0)
            normed(0, 1)
            exponentials(0, 3)
            squares(0, 2)
            transposed(0, 1, first_t[1])
            normed(0, 2)
            project(1, 0)
            project(1, 1, ps_t)
            squares(0, 3)
            transposed(0, 2, first_t[2])
            normed(0, 3)
            split_w_hi(0, 2)
            transposed(0, 3, first_t[3])

            exponentials(1, 0)
            split_w_hi(1, 0)
            exponentials(1, 1)
            squares(1, 0)
            split_w_hi(1, 1)
            normed(1, 0)
            router_tanh(0)
            hidden_tanh(0, 0)
            squares(1, 1)
            hidden_tanh(0, 1)
            split_g_hi(0, 0, 0)
            exponentials(1, 2)
            split_g_hi(0, 0, 1)
            transposed(1, 0)
            normed(1, 1)
            squares(1, 2)
            hidden_tanh(1, 0)
            split_w_hi(1, 2)
            transposed(1, 1)
            normed(1, 2)
            exponentials(1, 3)
            split_g_hi(1, 1, 0)
            hidden_tanh(1, 1)
            squares(1, 3)
            split_g_hi(1, 1, 1)
            transposed(1, 2)
            normed(1, 3)
            transposed(1, 3)

            def pair(b):
                n = 2 * b
                router_tanh(b)
                project(b + 1, 0)
                project(b + 1, 1, ps_t)
                hidden_tanh(n, 0)
                exponentials(b + 1, 0)
                split_g_hi(n, 0, 0)
                squares(b + 1, 0)
                exponentials(b + 1, 1)
                normed(b + 1, 0)
                hidden_tanh(n, 1)
                squares(b + 1, 1)
                split_g_hi(n, 0, 1)
                transposed(b + 1, 0)
                normed(b + 1, 1)
                exponentials(b + 1, 2)
                transposed(b + 1, 1)
                squares(b + 1, 2)
                normed(b + 1, 2)
                hidden_tanh(n + 1, 0)
                exponentials(b + 1, 3)
                split_g_hi(n + 1, 1, 0)
                transposed(b + 1, 2)
                squares(b + 1, 3)
                normed(b + 1, 3)
                hidden_tanh(n + 1, 1)
                split_g_hi(n + 1, 1, 1)
                transposed(b + 1, 3)

            with act.Fori(1, B - 1) as b:
                pair(b)
            router_tanh(B - 1)

            def hidden(n, par):
                hidden_tanh(n, 0)
                split_g_hi(n, par, 0)
                hidden_tanh(n, 1)
                split_g_hi(n, par, 1)

            with act.Fori(B - 1, B * E // 2) as u:
                hidden(2 * u, 0)
                hidden(2 * u + 1, 1)

        @block.vector
        def _(dve):
            def wait_apart(done, value):
                dve.wait_ge(done, value)
                if not isinstance(value, int):
                    dve.sem_inc(s_apart_dve, 1)

            def key_mask_row(b):
                if isinstance(b, int) and b < 1:
                    dve.wait_ge(s_masks_in, 32)
                else:
                    dve.wait_ge(s_neg, NT * b)
                dve.tensor_scalar(key_neg[:], key_u8[:, ds(b * S, S)], MASKED, None,
                                  ALU.mult).then_inc(s_key_neg, 1)

            def first_stats(b):
                if isinstance(b, int) and b == 0:
                    for t in range(NT):
                        dve.wait_ge(s_x0_in[t], 16)
                        dve.bn_stats(bn1[:, t, :], acc[:, t * D:(t + 1) * D]).then_inc(s_bn1, 1)
                        if t == 1:
                            key_mask_row(0)
                else:
                    wait_apart(s_x_in, 16 * b)
                    for t in range(NT):
                        dve.bn_stats(bn1[:, t, :], acc[:, ds((b * NT + t) * D, D)]).then_inc(s_bn1, 1)
                for t in range(NT):
                    wait_apart(s_bn1, b * NT + t + 1)
                    dve.bn_aggr(mv1[:, t, :], bn1[:, t, :]).then_inc(s_mv1, 1)
                dve.wait_ge(s_mv1, NT * (b + 1))
                dve.tensor_scalar(ve1[:], mv1[:, :, 1], EPS, None, ALU.add).then_inc(s_ve1, 1)

            def first_scale(b):
                dve.wait_ge(s_rstd1, b + 1)
                dve.tensor_scalar(rs1[:], rstd1[:], SCALING, None, ALU.mult).then_inc(s_rs1, 1)

            def masked_scores(b, t, bank=ps_s):
                tile = b * NT + t
                dve.wait_ge(s_scores, tile + 1)
                if not (isinstance(tile, int) and tile < 2):
                    dve.wait_ge(s_sq, tile - 1)
                dve.scalar_tensor_tensor(out=prob[:, t % 2, :], in0=acc[:, ds(tile * D, D)],
                                         scalar=mv1[:, t, 0:1], in1=bank[:], op0=ALU.subtract,
                                         op1=ALU.mult).then_inc(s_z, 1)
                dve.wait_ge(s_z, tile + 1)
                wait_apart(s_neg, tile + 1)
                dve.tensor_tensor_reduce(prob[:, t % 2, :], prob[:, t % 2, :], neg[:, t % 2, :], 1.0, LOWEST,
                                         ALU.add, ALU.max, zmax[:, t:t + 1]).then_inc(s_zmax, 1)

            def bias(b, t):
                dve.wait_ge(s_zmax, b * NT + t + 1)
                dve.wait_ge(s_rs1, b + 1)
                dve.scalar_tensor_tensor(out=nbias[:, t:t + 1], in0=zmax[:, t:t + 1], scalar=-1.0,
                                         in1=rs1[:, t:t + 1], op0=ALU.mult, op1=ALU.mult).then_inc(s_nb, 1)

            def scores(b, t, bank=ps_s):
                masked_scores(b, t, bank)
                bias(b, t)

            def split_first_w_lo(part):
                a, z = 2 * part, 2 * part + 2
                dve.wait_ge(s_whi, part + 1)
                dve.tensor_tensor(w_lo[:, 0, a:z, :], w_raw[:, a:z, :], w_hi[:, 0, a:z, :].bitcast(F32),
                                  ALU.subtract).then_inc(s_wlo0, 1)

            def residual(b, t):
                tile = b * NT + t
                row = acc[:, ds(tile * D, D)]
                dve.wait_ge(s_exp, tile + 1)
                dve.reciprocal(rden[:, t:t + 1], psum_row[:, t:t + 1]).then_inc(s_rden, 1)
                dve.wait_ge(s_rden, tile + 1)
                dve.tensor_scalar(rgain[:, t:t + 1], rden[:, t:t + 1], tg[:, 0:1], None,
                                  ALU.mult).then_inc(s_rgain, 1)
                dve.wait_ge(s_rgain, tile + 1)
                dve.scalar_tensor_tensor(out=row, in0=prob[:, t % 2, :], scalar=rgain[:, t:t + 1], in1=row,
                                         op0=ALU.mult, op1=ALU.add,
                                         accum_out=sum2[:, t:t + 1]).then_inc(s_x1, 1)
                dve.wait_ge(s_x1, tile + 1)
                dve.tensor_scalar(nmean2[:, t:t + 1], sum2[:, t:t + 1], -1.0 / D, None,
                                  ALU.mult).then_inc(s_nmean, 1)

            def logits(b, t, bank=ps_t):
                dve.wait_ge(s_logits, b * NT + t + 1)
                if t == 0 and not (isinstance(b, int) and b < 1):
                    dve.wait_ge(s_lt, b)
                dve.tensor_copy(lg[:, t, :], bank[:, 0:E]).then_inc(s_lg, 1)

            def router(b):
                step = [0]

                def done(ins):
                    step[0] += 1
                    ins.then_inc(s_rt, 1)
                    dve.wait_ge(s_rt, b * RT + step[0])

                full = [P, NT, E, E]
                dve.wait_ge(s_lt, b + 1)
                done(dve.tensor_scalar(sig[:], lt[:], 0.5, 0.5, ALU.mult, ALU.add))
                gate_bias = gb_sb[:, 2:2 + E].unsqueeze(1).to_broadcast([P, NT, E])
                done(dve.tensor_tensor(sc[:], sig[:], gate_bias, ALU.add))
                other = sc[:].unsqueeze(2).to_broadcast(full)
                own = sc[:].unsqueeze(3).to_broadcast(full)
                done(dve.tensor_tensor(above[:], other, own, ALU.is_gt))
                done(dve.tensor_tensor(ties[:], other, own, ALU.is_equal))
                done(dve.tensor_tensor(ties[:], ties[:], before[:].unsqueeze(1).to_broadcast(full), ALU.mult))
                done(dve.tensor_tensor(above[:], above[:], ties[:], ALU.add))
                done(dve.tensor_reduce(rank[:], above[:], AX_X, ALU.add))
                done(dve.scalar_tensor_tensor(out=picked[:], in0=rank[:], scalar=float(TOP_K), in1=sig[:],
                                              op0=ALU.is_lt, op1=ALU.mult))
                done(dve.tensor_reduce(wsum[:], picked[:], AX_X, ALU.add))
                done(dve.reciprocal(wrec[:], wsum[:]))
                dve.scalar_tensor_tensor(out=wts[:, ds(b * (NT * E), NT * E)].rearrange("p (t e) -> p t e", t=NT),
                                         in0=picked[:], scalar=half_gain[:],
                                         in1=wrec[:].unsqueeze(2).to_broadcast([P, NT, E]),
                                         op0=ALU.mult, op1=ALU.mult).then_inc(s_wts, 1)

            def gated(n, c):
                k = n * FC + c
                dve.wait_ge(s_th, k + 1)
                if not (isinstance(k, int) and k < FC):
                    dve.wait_ge(s_glo, k - FC + 1)
                dve.scalar_tensor_tensor(out=gate[:, c, :], in0=th[:, c, :], scalar=1.0, in1=ps_h[0][c][:],
                                         op0=ALU.add, op1=ALU.mult).then_inc(s_gate, 1)

            def times_h3(n, c):
                k = n * FC + c
                dve.wait_ge(s_h3, k + 1)
                dve.wait_ge(s_gate, k + 1)
                dve.tensor_tensor(gate[:, c, :], gate[:, c, :], ps_h[1][c][:], ALU.mult).then_inc(s_prod, 1)

            def add_output(n, e, g, t):
                dve.wait_ge(s_o, n * NT + t + 1)
                row = acc[:, ds((g * NT + t) * D, D)]
                dve.scalar_tensor_tensor(out=row, in0=ps_o[t % 2][:],
                                         scalar=wts[:, ds((g * NT + t) * E + e, 1)], in1=row,
                                         op0=ALU.mult, op1=ALU.add).then_inc(s_acc, 1)

            dve.wait_ge(s_tg, 1)
            dve.tensor_scalar(half_gain[:], tg[:, 1:2], 0.5, None, ALU.mult).then_inc(s_hg, 1)
            first_stats(0)
            masked_scores(0, 0, first_s[0])
            first_scale(0)
            bias(0, 0)
            scores(0, 1, first_s[1])
            residual(0, 0)
            split_first_w_lo(0)
            scores(0, 2, first_s[2])
            residual(0, 1)
            split_first_w_lo(1)
            scores(0, 3, first_s[3])
            residual(0, 2)
            logits(0, 0)
            key_mask_row(1)
            residual(0, 3)
            logits(0, 1, first_t[1])
            first_stats(1)
            first_scale(1)
            logits(0, 2, first_t[2])
            dve.wait_ge(s_hg, 1)
            dve.wait_ge(s_ident, 2)

            scores(1, 0)
            logits(0, 3, first_t[3])
            scores(1, 1, ps_t)
            residual(1, 0)
            gated(0, 0)
            residual(1, 1)
            times_h3(0, 0)
            gated(0, 1)
            scores(1, 2)
            times_h3(0, 1)
            residual(1, 2)
            logits(1, 0)
            gated(1, 0)
            scores(1, 3)
            times_h3(1, 0)
            residual(1, 3)
            logits(1, 1)
            gated(1, 1)
            times_h3(1, 1)
            router(0)
            dve.wait_ge(s_wts, 1)
            add_output(0, 0, 0, 0)
            add_output(0, 0, 0, 1)
            logits(1, 2)
            add_output(0, 0, 0, 2)
            add_output(0, 0, 0, 3)
            logits(1, 3)

            def pair(b):
                n = 2 * b
                key_mask_row(b + 1)
                first_stats(b + 1)
                gated(n, 0)
                masked_scores(b + 1, 0)
                first_scale(b + 1)
                bias(b + 1, 0)
                times_h3(n, 0)
                residual(b + 1, 0)
                scores(b + 1, 1)
                gated(n, 1)
                residual(b + 1, 1)
                times_h3(n, 1)
                add_output(n - 1, 1, b - 1, 0)
                add_output(n - 1, 1, b - 1, 1)
                scores(b + 1, 2)
                logits(b + 1, 0)
                add_output(n - 1, 1, b - 1, 2)
                residual(b + 1, 2)
                add_output(n - 1, 1, b - 1, 3)
                logits(b + 1, 1)
                router(b)
                gated(n + 1, 0)
                scores(b + 1, 3)
                times_h3(n + 1, 0)
                residual(b + 1, 3)
                gated(n + 1, 1)
                logits(b + 1, 2)
                times_h3(n + 1, 1)
                dve.wait_ge(s_wts, b + 1)
                for t in range(NT):
                    add_output(n, 0, b, t)
                logits(b + 1, 3)

            with dve.Fori(1, B - 1) as b:
                pair(b)
            router(B - 1)
            dve.wait_ge(s_wts, B)

            def unit(n, prev_n, prev_e, prev_g):
                for c in range(FC):
                    gated(n, c)
                    times_h3(n, c)
                for t in range(NT):
                    add_output(prev_n, prev_e, prev_g, t)

            unit(2 * B - 2, 2 * B - 3, 1, B - 2)
            unit(2 * B - 1, 2 * B - 2, 0, B - 1)
            unit(2 * B, 2 * B - 1, 1, B - 1)
            unit(2 * B + 1, 2 * B, 2, 0)
            unit(2 * B + 2, 2 * B + 1, 2, 1)
            unit(2 * B + 3, 2 * B + 2, 2, 2)
            with dve.Fori(3, E) as e:
                unit(B * e, B * e - 1, e - 1, B - 1)
                with dve.Fori(1, B) as g:
                    unit(B * e + g, B * e + g - 1, e, g - 1)
            for t in range(NT):
                add_output(LAST, E - 1, B - 1, t)

        @block.tensor
        def _(pe):
            def project(b, i, bank=ps_s):
                pe.wait_ge(s_ctx_in, 16 * (b + 1))
                if i == 0 and not (isinstance(b, int) and b == 0):
                    pe.wait_ge(s_z, NT * b)
                pe.matmul(bank[:], wqk_sb[:, i * P:(i + 1) * P], ctx_sb[:], start=True,
                          stop=True).then_inc(s_proj, 1)

            def scores(b, t, bank=ps_s, skipped=0):
                pe.wait_ge(s_qk, 2 * b + 2)
                if t > 0 and bank is ps_s and not (isinstance(b, int) and b == 0):
                    pe.wait_ge(s_z, b * NT + t - skipped)
                pe.matmul(bank[:], q_sb[:, t * P:(t + 1) * P], k_sb[:], start=True,
                          stop=True).then_inc(s_scores, 1)

            def transpose(b, t, bank=ps_t):
                tile = b * NT + t
                pe.wait_ge(s_xn, tile + 1)
                if not (isinstance(b, int) and b == 0):
                    pe.wait_ge(s_lg, tile)
                for k in range(KC):
                    mm = pe.transpose(bank[:, k * P:(k + 1) * P], xn[:, k * P:(k + 1) * P], ident[:])
                mm.then_inc(s_xpose, 1)

            def logits(b, t, bank=ps_t):
                pe.wait_ge(s_xt32, b * NT + t + 1)
                pe.wait_ge(s_xhi, b * NT + t + 1)
                for k in range(KC):
                    mm = pe.matmul(bank[:, 0:E], xt_f32[:, k, :], wg_sb[:, k, :], start=(k == 0),
                                   stop=(k == KC - 1))
                mm.then_inc(s_logits, 1)

            def hidden(n, slot, g, c, m, half=None):
                kk = n * FC + c
                if not (isinstance(n, int) and n == 0):
                    pe.wait_ge((s_gate, s_prod)[m], kk - FC + 1)
                a, size = (0, S) if half is None else (half * (S // 2), S // 2)
                bank = ps_h[m][c][:, a:a + size]
                for k in range(KC):
                    w = slice(k * P, (k + 1) * P)
                    hi = w_hi[:, slot, 2 * c + m, w]
                    lo = w_lo[:, slot, 2 * c + m, w]
                    x_hi = xt_hi[:, ds(g * GRP + (k * S + a), size)]
                    x_lo = xt_lo[:, ds(g * GRP + (k * S + a), size)]
                    pe.matmul(bank, hi, x_hi, start=(k == 0), stop=False)
                    pe.matmul(bank, hi, x_lo, start=False, stop=False)
                    mm = pe.matmul(bank, lo, x_hi, start=False, stop=(k == KC - 1))
                if half != 0:
                    mm.then_inc((s_h1, s_h3)[m], 1)

            def output(n, par, slot, t):
                if t == 0:
                    pe.wait_ge(s_ghi, FC * (n + 1))
                    pe.wait_ge(s_glo, FC * (n + 1))
                if not (isinstance(n, int) and n == 0 and t < 2):
                    pe.wait_ge(s_acc, n * NT + t - 1)
                bank = ps_o[t % 2]
                tok = slice(t * P, (t + 1) * P)
                for c in range(FC):
                    pe.matmul(bank[:], g_hi[:, par, c, tok], w_hi[:, slot, 2 * FC + c, :],
                              start=(c == 0), stop=False)
                    pe.matmul(bank[:], g_hi[:, par, c, tok], w_lo[:, slot, 2 * FC + c, :],
                              start=False, stop=False)
                    mm = pe.matmul(bank[:], g_lo[:, par, c, tok], w_hi[:, slot, 2 * FC + c, :],
                                   start=False, stop=(c == FC - 1))
                mm.then_inc(s_o, 1)

            pe.wait_ge(s_wqk_in, 16)
            pe.wait_ge(s_ident, 2)
            project(0, 0)
            project(0, 1, ps_o[0])
            scores(0, 0, first_s[0])
            scores(0, 1, first_s[1])
            scores(0, 2, first_s[2])
            pe.wait_ge(s_z, 1)
            scores(0, 3, first_s[3])
            pe.wait_ge(s_wg_in, 16)
            transpose(0, 0)
            logits(0, 0)
            transpose(0, 1, first_t[1])
            logits(0, 1, first_t[1])
            pe.wait_ge(s_lg, 2)
            project(1, 0)
            pe.wait_ge(s_xlo, 2)
            pe.wait_ge(s_wlo0, 1)
            hidden(0, 0, 0, 0, 0, half=0)
            project(1, 1, ps_t)
            transpose(0, 2, first_t[2])
            hidden(0, 0, 0, 0, 1, half=0)
            logits(0, 2, first_t[2])
            pe.wait_ge(s_wlo0, 2)
            hidden(0, 0, 0, 1, 0, half=0)
            transpose(0, 3, first_t[3])
            scores(1, 0)
            hidden(0, 0, 0, 1, 1, half=0)
            logits(0, 3, first_t[3])
            scores(1, 1, ps_t)

            pe.wait_ge(s_xlo, 4)
            hidden(0, 0, 0, 0, 0, half=1)
            hidden(0, 0, 0, 0, 1, half=1)
            scores(1, 2, skipped=1)
            hidden(0, 0, 0, 1, 0, half=1)
            hidden(0, 0, 0, 1, 1, half=1)
            pe.wait_ge(s_wlo, wlo_count(1, 0))
            hidden(1, 1, 0, 0, 0)
            pe.wait_ge(s_z, NT + 2)
            transpose(1, 0)
            hidden(1, 1, 0, 0, 1)
            logits(1, 0)
            scores(1, 3)
            pe.wait_ge(s_wlo, wlo_count(1, 1))
            hidden(1, 1, 0, 1, 0)
            transpose(1, 1)
            hidden(1, 1, 0, 1, 1)
            logits(1, 1)
            pe.wait_ge(s_lg, 4)
            output(0, 0, 0, 0)
            transpose(1, 2)
            output(0, 0, 0, 1)
            logits(1, 2)
            output(0, 0, 0, 2)
            transpose(1, 3)
            output(0, 0, 0, 3)
            logits(1, 3)
            pe.wait_ge(s_wlo, wlo_count(1, 2))

            def pair(b):
                n = 2 * b
                pe.wait_ge(s_xhi, NT * (b + 1))
                pe.wait_ge(s_xlo, NT * (b + 1))
                project(b + 1, 0)
                pe.wait_ge(s_lg, NT * (b + 1))
                project(b + 1, 1, ps_t)
                hidden(n, 0, b, 0, 0)
                scores(b + 1, 0)
                hidden(n, 0, b, 0, 1)
                scores(b + 1, 1)
                hidden(n, 0, b, 1, 0)
                hidden(n, 0, b, 1, 1)
                output(n - 1, 1, 1, 0)
                transpose(b + 1, 0)
                output(n - 1, 1, 1, 1)
                scores(b + 1, 2)
                logits(b + 1, 0)
                output(n - 1, 1, 1, 2)
                transpose(b + 1, 1)
                output(n - 1, 1, 1, 3)
                logits(b + 1, 1)
                hidden(n + 1, 1, b, 0, 0)
                scores(b + 1, 3)
                hidden(n + 1, 1, b, 0, 1)
                transpose(b + 1, 2)
                hidden(n + 1, 1, b, 1, 0)
                logits(b + 1, 2)
                hidden(n + 1, 1, b, 1, 1)
                output(n, 0, 0, 0)
                transpose(b + 1, 3)
                output(n, 0, 0, 1)
                logits(b + 1, 3)
                output(n, 0, 0, 2)
                output(n, 0, 0, 3)

            with pe.Fori(1, B - 1) as b:
                pair(b)
            pe.wait_ge(s_xhi, NT * B)
            pe.wait_ge(s_xlo, NT * B)

            def unit(n, slot, g, prev_n, prev_par, prev_slot):
                for c in range(FC):
                    hidden(n, slot, g, c, 0)
                    hidden(n, slot, g, c, 1)
                for t in range(NT):
                    output(prev_n, prev_par, prev_slot, t)

            unit(2 * B - 2, 0, B - 1, 2 * B - 3, 1, 1)
            unit(2 * B - 1, 1, B - 1, 2 * B - 2, 0, 0)
            with pe.Fori(1, E // 2) as p:
                for slot in range(2):
                    n = p * (2 * B) + slot * B
                    pe.wait_ge(s_wlo, wlo_count(p * 2 + slot, 1))
                    unit(n, slot, 0, n - 1, 1, 1 - slot)
                    pe.wait_ge(s_wlo, wlo_count(p * 2 + slot, 2))
                    unit(n + 1, slot, 1, n, 0, slot)
                    unit(n + 2, slot, 2, n + 1, 1, slot)
                    unit(n + 3, slot, 3, n + 2, 0, slot)
            for t in range(NT):
                output(LAST, 1, 1, t)


def kernel(x, ctx_512, mask_SxS2_bk1, mask_BxS2_bf0, g_xattn, g_ffn, L0_xattn_Wq, L0_xattn_bq, L0_xattn_Wk,
           L0_xattn_bk, L0_ffn_Wg, L0_ffn_W1, L0_ffn_W2, L0_ffn_W3, L0_ffn_bias):
    import numpy as np
    import concourse.bacc as bacc
    from concourse.bass_utils import run_bass_kernel_spmd

    x = np.asarray(x)
    B, S, D = x.shape
    E, F, _ = L0_ffn_W1.shape
    fc, kc = F // P, D // P

    def hidden_layout(w):
        w = np.asarray(w).reshape(E, fc, P, kc, P).transpose(0, 4, 1, 3, 2)
        return w.reshape(E, P, fc, 1, D)

    w13 = np.concatenate([hidden_layout(L0_ffn_W1), hidden_layout(L0_ffn_W3)], axis=3).reshape(E, P, 2 * fc, D)
    w2 = np.asarray(L0_ffn_W2).reshape(E, D, fc, P).transpose(0, 3, 2, 1)
    arrays = {
        "x": x,
        "ctx_t": np.asarray(ctx_512).transpose(0, 2, 1),
        "wqk_t": np.concatenate([np.asarray(L0_xattn_Wq).T, np.asarray(L0_xattn_Wk).T], axis=1),
        "bqk": np.stack([np.asarray(L0_xattn_bq), np.asarray(L0_xattn_bk)], axis=1),
        "gains_bias": np.concatenate([np.asarray(g_xattn), np.asarray(g_ffn), np.asarray(L0_ffn_bias)]),
        "attn_mask": np.asarray(mask_SxS2_bk1),
        "key_mask": np.asarray(mask_BxS2_bf0).reshape(-1),
        "wg_t": np.asarray(L0_ffn_Wg).reshape(E, kc, P).transpose(2, 1, 0),
        "experts": np.concatenate([w13, w2], axis=2),
    }
    arrays = {f"in_{n}": np.ascontiguousarray(a) for n, a in arrays.items()}
    nc = bacc.Bacc("TRN2", target_bir_lowering=False, num_devices=1)
    ins = [nc.dram_tensor(n, a.shape, mybir.dt.from_np(a.dtype), kind="ExternalInput").ap()
           for n, a in arrays.items()]
    out = nc.dram_tensor("out", (B * S // P, P, D), F32, kind="ExternalOutput").ap()
    flamingo_gated_block(nc, *ins, out)
    r = run_bass_kernel_spmd(nc, [arrays], core_ids=[0])
    return r.results[0]["out"].reshape(B, S, D)
```

```python
from contextlib import ExitStack

import concourse.bass as bass
from concourse import mybir

F32 = mybir.dt.float32
F32R = mybir.dt.float32r
BF16 = mybir.dt.bfloat16
U8 = mybir.dt.uint8
ALU = mybir.AluOpType
ACT = mybir.ActivationFunctionType
AX_X = mybir.AxisListType.X
ds = bass.ds

P = 128
EPS = 1e-5
TOP_K = 2
MASKED = -1e30
LOWEST = -1e29


def flamingo_gated_block(nc, x, ctx_t, wqk_t, bqk, gains_bias, attn_mask, key_mask, wg_t, experts, out):
    B, S, D = x.shape
    E = experts.shape[0]
    KC = D // P
    NT = S // P
    PIECES = experts.shape[2]
    FC = PIECES // 3
    PARTS = 3
    GRP = KC * S
    SLOT = PIECES * D
    LAST = B * E - 1
    SCALING = float(P) ** -0.5
    assert (B, S, D, E, FC) == (4, 512, 512, 8, 2)

    with ExitStack() as ctx:
        def sb(name, shape, dt=F32):
            return ctx.enter_context(nc.sbuf_tensor(name, shape, dt))

        def psum(name, shape=(P, 512)):
            return ctx.enter_context(nc.psum_tensor(name, list(shape), F32))

        def sem(name):
            return ctx.enter_context(nc.semaphore(name))

        acc = sb("acc", [P, B * NT * D])
        xt_hi = sb("xt_hi", [P, B * GRP], F32R)
        xt_lo = sb("xt_lo", [P, B * GRP], F32R)
        w_hi = sb("w_hi", [P, 2, PIECES, D], F32R)
        w_lo = sb("w_lo", [P, 2, PIECES, D], F32R)
        w_raw = sb("w_raw", [P, PIECES, D])
        g_hi = sb("g_hi", [P, 2, FC, S], F32R)
        g_lo = sb("g_lo", [P, 2, FC, S], F32R)
        th = sb("th", [P, FC, S])
        gate = sb("gate", [P, FC, S])
        ctx_sb = sb("ctx_sb", [P, S])
        wqk_sb = sb("wqk_sb", [P, 2 * P])
        bqk_sb = sb("bqk_sb", [P, 2])
        q_sb = sb("q_sb", [P, S])
        k_sb = sb("k_sb", [P, S])
        attn_neg = sb("attn_neg", [P, NT, S], BF16)
        key_u8 = sb("key_u8", [P, B * S], U8)
        key_neg = sb("key_neg", [P, S], BF16)
        neg = sb("neg", [P, 2, S], BF16)
        prob = sb("prob", [P, 2, S])
        xn = sb("xn", [P, D])
        xt_f32 = sb("xt_f32", [P, KC, P])
        ident = sb("ident", [P, P])
        attn_u8 = gate[:, 0, :].bitcast(U8).rearrange("p (t s) -> p t s", t=NT)
        bn1 = sb("bn1", [P, NT, 6])
        mv1 = sb("mv1", [P, NT, 2])
        ve1 = sb("ve1", [P, NT])
        rstd1 = sb("rstd1", [P, NT])
        rs1 = sb("rs1", [P, NT])
        zmax = sb("zmax", [P, NT])
        nbias = sb("nbias", [P, NT])
        psum_row = sb("psum_row", [P, NT])
        rden = sb("rden", [P, NT])
        rgain = sb("rgain", [P, NT])
        sum2 = sb("sum2", [P, NT])
        nmean2 = sb("nmean2", [P, NT])
        sqsum2 = sb("sqsum2", [P, NT])
        ve2 = sb("ve2", [P, NT])
        shift2 = sb("shift2", [P, NT])
        rstd2 = sb("rstd2", [P, NT])
        minus_half = sb("minus_half", [P, NT])
        gb_sb = sb("gb_sb", [P, 2 + E])
        tg = sb("tg", [P, 2])
        half_gain = sb("half_gain", [P, 1])
        wg_sb = sb("wg_sb", [P, KC, E])
        wg_split = sb("wg_split", [P, KC, 2, E], F32R)
        add_parts = sb("add_parts", [P, E])
        sig = sb("sig", [P, NT, E])
        sc = sb("sc", [P, NT, E])
        before = sb("before", [P, E, E], BF16)
        above = sb("above", [P, NT, E, E], BF16)
        ties = sb("ties", [P, NT, E, E], BF16)
        rank = sb("rank", [P, NT, E])
        picked = sc
        wsum = sb("wsum", [P, NT])
        wrec = sb("wrec", [P, NT])
        wts = sb("wts", [P, B * NT * E])

        both_logits = xt_f32[0:2 * E].rearrange("p k s -> p (k s)")

        ps_h = [[psum(f"ps_h{m}_{c}") for c in range(FC)] for m in (1, 3)]
        ps_o = [psum(f"ps_o{i}") for i in range(2)]
        ps_s = psum("ps_s")
        ps_t = psum("ps_t")
        first_s = [ps_o[1], ps_s, ps_o[0], ps_o[1]]
        first_t = [ps_t, ps_s, ps_o[0], ps_o[1]]

        s_wqk_in = sem("s_wqk_in")
        s_bqk_in = sem("s_bqk_in")
        s_gains_in = sem("s_gains_in")
        s_wg_in = sem("s_wg_in")
        s_x0_in = [sem(f"s_x0_in{t}") for t in range(NT)]
        s_masks_in = sem("s_masks_in")
        s_ctx_in = sem("s_ctx_in")
        s_x_in = sem("s_x_in")
        s_w_in = [sem(f"s_w_in{part}") for part in range(PARTS)]
        s_out = sem("s_out")
        s_zero = sem("s_zero")
        s_ident = sem("s_ident")
        s_half = sem("s_half")
        s_attn_neg = sem("s_attn_neg")
        s_neg = sem("s_neg")
        s_rstd1 = sem("s_rstd1")
        s_ve2 = sem("s_ve2")
        s_rstd2 = sem("s_rstd2")
        s_shift2 = sem("s_shift2")
        s_xlo = sem("s_xlo")
        s_glo = sem("s_glo")
        s_whi = sem("s_whi")
        s_wlo = sem("s_wlo")
        s_proj = sem("s_proj")
        s_scores = sem("s_scores")
        s_xpose = sem("s_xpose")
        s_both_logits = sem("s_both_logits")
        s_logits = sem("s_logits")
        s_first = sem("s_first")
        s_h1 = sem("s_h1")
        s_h3 = sem("s_h3")
        s_o = sem("s_o")
        s_tg = sem("s_tg")
        s_qk = sem("s_qk")
        s_exp = sem("s_exp")
        s_sq = sem("s_sq")
        s_xn = sem("s_xn")
        s_xt32 = sem("s_xt32")
        s_xhi = sem("s_xhi")
        s_logits_out = sem("s_logits_out")
        s_lt = sem("s_lt")
        s_th = sem("s_th")
        s_ghi = sem("s_ghi")
        s_bn1 = sem("s_bn1")
        s_mv1 = sem("s_mv1")
        s_ve1 = sem("s_ve1")
        s_rs1 = sem("s_rs1")
        s_z = sem("s_z")
        s_zmax = sem("s_zmax")
        s_nb = sem("s_nb")
        s_rden = sem("s_rden")
        s_rgain = sem("s_rgain")
        s_x1 = sem("s_x1")
        s_nmean = sem("s_nmean")
        s_key_neg = sem("s_key_neg")
        s_wg_hi = sem("s_wg_hi")
        s_wg_lo = sem("s_wg_lo")
        s_rt = sem("s_rt")
        s_wts = sem("s_wts")
        s_hg = sem("s_hg")
        s_whi01 = sem("s_whi01")
        s_wlo01 = sem("s_wlo01")
        s_gate = sem("s_gate")
        s_prod = sem("s_prod")
        s_acc = sem("s_acc")

        s_apart_dve = sem("s_apart_dve")
        s_apart_pool = sem("s_apart_pool")
        s_apart_act = sem("s_apart_act")

        def split_count(e, part):
            if isinstance(e, int) and e < 2:
                return e + 1
            return PARTS * (e - 1) + part

        def scale_count(b, t):
            return 1 if isinstance(b, int) and b == 0 and t == 0 else b + 2

        def row_buffer(b, t):
            if isinstance(b, int) and b == 0 and t >= 2:
                return th[:, t - 2, :]
            return prob[:, t % 2, :]

        def transposed_f32(b, t):
            if isinstance(b, int) and b == 0 and t < 2:
                return gate[:, t, :].rearrange("p (k s) -> p k s", k=KC)
            if isinstance(b, int) and b == 0 and t == 2:
                return prob[:, 0, :].rearrange("p (k s) -> p k s", k=KC)
            return xt_f32[:]

        WARM = (24, 4)
        RT = 10

        block = ctx.enter_context(nc.Block())

        @block.sync
        def _(sp):
            def load_ctx(b):
                sp.dma_start(ctx_sb[:], ctx_t[ds(b, 1)].rearrange("a p n -> p (a n)")).then_inc(s_ctx_in, 16)

            def load_x(b):
                sp.dma_start(acc[:, ds(b * (NT * D), NT * D)].rearrange("p (t n) -> p t n", t=NT),
                             x[ds(b, 1)].rearrange("a (t p) n -> p (a t) n", p=P)).then_inc(s_x_in, 16)

            def load_w(e, part):
                a, z = 2 * part, 2 * part + 2
                sp.dma_start(w_raw[:, a:z, :], experts[ds(e, 1), :, a:z, :].rearrange("a p m n -> p (a m) n")).then_inc(
                    s_w_in[part], 16)

            sp.dma_start(wqk_sb[:], wqk_t).then_inc(s_wqk_in, 16)
            load_ctx(0)
            sp.dma_start(bqk_sb[:], bqk).then_inc(s_bqk_in, 16)
            sp.dma_start(gb_sb[:], gains_bias.partition_broadcast(P)).then_inc(s_gains_in, 16)
            for t in range(NT):
                sp.dma_start(acc[:, t * D:(t + 1) * D], x[0, t * P:(t + 1) * P, :]).then_inc(s_x0_in[t], 16)
                if t == 0:
                    sp.dma_start(key_u8[:], key_mask.partition_broadcast(P)).then_inc(s_masks_in, 16)
                    sp.dma_start(attn_u8, attn_mask.rearrange("(t p) n -> p t n", p=P)).then_inc(s_masks_in, 16)
            load_w(0, 0)
            load_w(0, 1)
            sp.dma_start(wg_sb[:], wg_t).then_inc(s_wg_in, 16)
            load_w(0, 2)
            load_x(1)
            sp.wait_ge(s_proj, 2)
            load_ctx(1)
            for part in range(PARTS):
                if part < 2:
                    sp.wait_ge(s_wlo01, part + 1)
                    sp.wait_ge(s_first, part + 1)
                else:
                    sp.wait_ge(s_wlo, split_count(0, part))
                load_w(1, part)
            with sp.Fori(2, B) as b:
                sp.wait_ge(s_x_in, 16 * b - 16)
                load_x(b)
                sp.wait_ge(s_proj, 2 * b)
                load_ctx(b)
            for part in range(PARTS):
                if part < 2:
                    sp.wait_ge(s_wlo01, 2 + part + 1)
                else:
                    sp.wait_ge(s_wlo, split_count(1, part))
                load_w(2, part)
            with sp.Fori(3, E) as e:
                for part in range(PARTS):
                    sp.wait_ge(s_wlo, split_count(e - 1, part))
                    load_w(e, part)

            def store_tile(tile, t):
                sp.dma_start(out[ds(tile, 1)].rearrange("a p n -> p (a n)"),
                             acc[:, ds(tile * D, D)]).then_inc(s_out, 16)

            with sp.Fori(0, B) as g:
                for t in range(NT):
                    sp.wait_ge(s_acc, (g + B * (E - 1)) * NT + t + 1)
                    store_tile(g * NT + t, t)
            sp.wait_ge(s_out, 16 * B * NT)

        @block.gpsimd
        def _(pool):
            def wait_apart(done, value):
                pool.wait_ge(done, value)
                if not isinstance(value, int):
                    pool.sem_inc(s_apart_pool, 1)

            def masks(b, t):
                tile = b * NT + t
                pool.wait_ge(s_key_neg, b + 1)
                if isinstance(b, int) and b == 0:
                    pool.wait_ge(s_attn_neg, t + 1)
                if not (isinstance(tile, int) and tile < 2):
                    pool.wait_ge(s_zmax, tile - 1)
                pool.tensor_tensor(neg[:, t % 2, :], attn_neg[:, t, :], key_neg[:], ALU.add).then_inc(s_neg, 1)

            def rstd_first(b, a=0, z=NT):
                pool.wait_ge(s_ve1, scale_count(b, z - 1))
                pool.tensor_tensor(rstd1[:, a:z], ve1[:, a:z], minus_half[:, a:z], ALU.pow).then_inc(s_rstd1, 1)

            def rstd_second(b, t):
                tile = b * NT + t
                col = slice(t, t + 1)
                wait_apart(s_sq, tile + 1)
                pool.tensor_scalar(ve2[:, col], sqsum2[:, col], 1.0 / D, EPS, ALU.mult, ALU.add).then_inc(s_ve2, 1)
                pool.wait_ge(s_ve2, tile + 1)
                pool.tensor_tensor(rstd2[:, col], ve2[:, col], minus_half[:, col], ALU.pow).then_inc(s_rstd2, 1)
                pool.wait_ge(s_rstd2, tile + 1)
                pool.tensor_tensor(shift2[:, col], rstd2[:, col], nmean2[:, col], ALU.mult).then_inc(s_shift2, 1)

            def split_x_lo(b, t):
                tile = b * NT + t
                pool.wait_ge(s_xhi, tile + 1)
                cols = (slice(None), slice(None), slice(t * P, (t + 1) * P))
                hi = xt_hi[:, ds(b * GRP, GRP)].rearrange("p (k s) -> p k s", k=KC)[cols]
                lo = xt_lo[:, ds(b * GRP, GRP)].rearrange("p (k s) -> p k s", k=KC)[cols]
                pool.tensor_tensor(lo, transposed_f32(b, t), hi.bitcast(F32), ALU.subtract).then_inc(s_xlo, 1)

            def split_g_lo(n, par, c):
                pool.wait_ge(s_ghi, n * FC + c + 1)
                pool.tensor_tensor(g_lo[:, par, c, :], gate[:, c, :], g_hi[:, par, c, :].bitcast(F32),
                                   ALU.subtract).then_inc(s_glo, 1)

            def split_w_lo(e, slot, part):
                a, z = 2 * part, 2 * part + 2
                pool.wait_ge(s_whi, split_count(e, part))
                pool.tensor_tensor(w_lo[:, slot, a:z, :], w_raw[:, a:z, :], w_hi[:, slot, a:z, :].bitcast(F32),
                                   ALU.subtract).then_inc(s_wlo, 1)

            def split_w(e, slot, part):
                a, z = 2 * part, 2 * part + 2
                wait_apart(s_w_in[part], 16 * (e + 1))
                pool.tensor_copy(w_hi[:, slot, a:z, :], w_raw[:, a:z, :]).then_inc(s_whi, 1)
                split_w_lo(e, slot, part)

            pool.memset(ident[:], 0.0).then_inc(s_zero, 1)
            pool.memset(before[:], 1.0).then_inc(s_zero, 1)
            pool.memset(add_parts[:], 0.0).then_inc(s_zero, 1)
            pool.memset(minus_half[:], -0.5).then_inc(s_half, 1)
            pool.wait_ge(s_zero, 3)
            pool.affine_select(out=ident[:], in_=ident[:], compare_op=ALU.not_equal, fill=1.0, base=0,
                               pattern=[[-1, P]], channel_multiplier=1).then_inc(s_ident, 1)
            pool.affine_select(out=before[:], in_=before[:], compare_op=ALU.is_gt, fill=0.0, base=0,
                               pattern=[[1, E], [-1, E]], channel_multiplier=0).then_inc(s_ident, 1)
            for part in range(2):
                if part:
                    pool.wait_ge(s_ident, 3)
                pool.affine_select(out=add_parts[:], in_=add_parts[:], compare_op=ALU.not_equal, fill=1.0,
                                   base=-part * E, pattern=[[-1, E]], channel_multiplier=1).then_inc(s_ident, 1)
            pool.wait_ge(s_half, 1)

            rstd_first(0, 0, 1)
            masks(0, 0)
            masks(0, 1)
            rstd_first(0, 1, NT)
            masks(0, 2)
            rstd_second(0, 0)
            masks(0, 3)
            rstd_second(0, 1)
            rstd_second(0, 2)
            split_x_lo(0, 0)
            rstd_second(0, 3)
            split_x_lo(0, 1)
            split_x_lo(0, 2)

            rstd_first(1)
            split_x_lo(0, 3)
            masks(1, 0)
            masks(1, 1)
            masks(1, 2)
            split_g_lo(0, 0, 0)
            rstd_second(1, 0)
            split_w_lo(0, 0, 2)
            rstd_second(1, 1)
            masks(1, 3)
            split_g_lo(0, 0, 1)
            split_x_lo(1, 0)
            rstd_second(1, 2)
            split_x_lo(1, 1)
            rstd_second(1, 3)
            split_x_lo(1, 2)
            split_g_lo(1, 1, 0)
            split_x_lo(1, 3)
            split_g_lo(1, 1, 1)
            split_w_lo(1, 1, 2)

            def pair(b):
                masks(b + 1, 0)
                rstd_first(b + 1)
                masks(b + 1, 1)
                masks(b + 1, 2)
                rstd_second(b + 1, 0)
                split_g_lo(2 * b, 0, 0)
                masks(b + 1, 3)
                rstd_second(b + 1, 1)
                split_g_lo(2 * b, 0, 1)
                split_x_lo(b + 1, 0)
                split_x_lo(b + 1, 1)
                rstd_second(b + 1, 2)
                split_g_lo(2 * b + 1, 1, 0)
                rstd_second(b + 1, 3)
                split_x_lo(b + 1, 2)
                split_g_lo(2 * b + 1, 1, 1)
                split_x_lo(b + 1, 3)

            with pool.Fori(1, B - 1) as b:
                pair(b)
            n = 2 * (B - 1)
            split_g_lo(n, 0, 0)
            split_g_lo(n, 0, 1)
            pool.wait_ge(s_h3, FC * (n + 1))
            split_w(2, 0, 0)
            split_g_lo(n + 1, 1, 0)
            split_w(2, 0, 1)
            split_g_lo(n + 1, 1, 1)
            pool.wait_ge(s_o, NT * (n + 1))
            split_w(2, 0, 2)

            def expert(e, slot, loads_next):
                for g in range(B):
                    n = B * e + g
                    if loads_next and g > 0:
                        if g == 1:
                            wait_apart(s_o, NT * B * e)
                        split_w(e + 1, 1 - slot, g - 1)
                    split_g_lo(n, g % 2, 0)
                    split_g_lo(n, g % 2, 1)

            with pool.Fori(1, E // 2 - 1) as p:
                for slot in range(2):
                    expert(2 * p + slot, slot, True)
            expert(E - 2, 0, True)
            expert(E - 1, 1, False)

        @block.scalar
        def _(act):
            def wait_apart(done, value):
                act.wait_ge(done, value)
                if not isinstance(value, int):
                    act.sem_inc(s_apart_act, 1)

            def project(b, i, bank=ps_s):
                act.wait_ge(s_proj, 2 * b + i + 1)
                act.activation((q_sb, k_sb)[i][:], bank[:], ACT.Identity,
                               bias=bqk_sb[:, i:i + 1]).then_inc(s_qk, 1)

            def exponentials(b, t):
                act.wait_ge(s_nb, b * NT + t + 1)
                act.activation(row_buffer(b, t), row_buffer(b, t), ACT.Exp, bias=nbias[:, t:t + 1],
                               scale=rs1[:, t:t + 1], accum_out=psum_row[:, t:t + 1]).then_inc(s_exp, 1)

            def squares(b, t):
                tile = b * NT + t
                wait_apart(s_nmean, tile + 1)
                act.activation(row_buffer(b, t), acc[:, ds(tile * D, D)], ACT.Square,
                               bias=nmean2[:, t:t + 1], accum_out=sqsum2[:, t:t + 1]).then_inc(s_sq, 1)

            def normed(b, t):
                tile = b * NT + t
                if not (isinstance(tile, int) and tile < 1):
                    act.wait_ge(s_xpose, tile)
                wait_apart(s_shift2, tile + 1)
                act.activation(xn[:], acc[:, ds(tile * D, D)], ACT.Identity, bias=shift2[:, t:t + 1],
                               scale=rstd2[:, t:t + 1]).then_inc(s_xn, 1)

            def transposed_whole(b, t, bank=ps_t):
                tile = b * NT + t
                act.wait_ge(s_xpose, tile + 1)
                if not (isinstance(tile, int) and tile < 4):
                    act.wait_ge(s_xlo, tile)
                    if t == 0:
                        act.wait_ge(s_logits, b)
                act.copy(transposed_f32(b, t), bank[:].rearrange("p (k s) -> p k s", k=KC)).then_inc(s_xt32, 1)

            def transposed_hi(b, t, bank=ps_t):
                act.copy(xt_hi[:, ds(b * GRP, GRP)].rearrange("p (k s) -> p k s", k=KC)[:, :, t * P:(t + 1) * P],
                         bank[:].rearrange("p (k s) -> p k s", k=KC)).then_inc(s_xhi, 1)

            def transposed(b, t, bank=ps_t):
                transposed_whole(b, t, bank)
                transposed_hi(b, t, bank)

            def attention_mask(t):
                if t == 0:
                    act.wait_ge(s_masks_in, 32)
                act.activation(attn_neg[:, t, :], attn_u8[:, t, :], ACT.Copy, scale=MASKED).then_inc(s_attn_neg, 1)

            def logits_out(b, bank=ps_t):
                act.wait_ge(s_both_logits, b + 1)
                act.copy(both_logits, bank[0:2 * E, :]).then_inc(s_logits_out, 1)

            def router_tanh(b, bank=ps_t):
                act.wait_ge(s_logits, b + 1)
                if not (isinstance(b, int) and b == 0):
                    act.wait_ge(s_wts, b)
                act.activation(sig[:], bank[:, 0:NT * E].rearrange("p (t e) -> p t e", t=NT), ACT.Tanh,
                               scale=0.5).then_inc(s_lt, 1)

            def hidden_tanh(n, c):
                k = n * FC + c
                act.wait_ge(s_h1, k + 1)
                if not (isinstance(k, int) and k < FC):
                    act.wait_ge(s_gate, k - FC + 1)
                act.activation(th[:, c, :], ps_h[0][c][:], ACT.Tanh, scale=0.5).then_inc(s_th, 1)

            def split_g_hi(n, par, c):
                k = n * FC + c
                act.wait_ge(s_prod, k + 1)
                if not (isinstance(n, int) and n < 2):
                    act.wait_ge(s_o, NT * (n - 1))
                act.copy(g_hi[:, par, c, :], gate[:, c, :]).then_inc(s_ghi, 1)

            def split_w_hi(slot, part):
                a, z = 2 * part, 2 * part + 2
                act.wait_ge(s_w_in[part], 16 * (slot + 1))
                act.copy(w_hi[:, slot, a:z, :], w_raw[:, a:z, :]).then_inc(s_whi, 1)

            act.wait_ge(s_gains_in, 16)
            act.activation(tg[:], gb_sb[:, 0:2], ACT.Tanh).then_inc(s_tg, 1)
            act.wait_ge(s_bqk_in, 16)
            project(0, 0)
            attention_mask(0)
            attention_mask(1)
            project(0, 1, ps_o[0])
            attention_mask(2)
            attention_mask(3)
            exponentials(0, 0)
            squares(0, 0)
            exponentials(0, 1)
            normed(0, 0)
            exponentials(0, 2)
            transposed_whole(0, 0)
            squares(0, 1)
            exponentials(0, 3)
            normed(0, 1)
            squares(0, 2)
            transposed_whole(0, 1, first_t[1])
            squares(0, 3)
            normed(0, 2)
            transposed_hi(0, 0)
            transposed_hi(0, 1, first_t[1])
            transposed(0, 2, first_t[2])
            project(1, 0)
            normed(0, 3)
            project(1, 1, ps_t)
            transposed(0, 3, first_t[3])

            exponentials(1, 0)
            hidden_tanh(0, 0)
            exponentials(1, 1)
            logits_out(0, ps_o[0])
            split_g_hi(0, 0, 0)
            squares(1, 0)
            hidden_tanh(0, 1)
            normed(1, 0)
            split_w_hi(0, 2)
            router_tanh(0, ps_o[0])
            squares(1, 1)
            transposed(1, 0)
            exponentials(1, 2)
            normed(1, 1)
            split_g_hi(0, 0, 1)
            hidden_tanh(1, 0)
            exponentials(1, 3)
            transposed(1, 1)
            squares(1, 2)
            hidden_tanh(1, 1)
            split_g_hi(1, 1, 0)
            normed(1, 2)
            squares(1, 3)
            transposed(1, 2)
            normed(1, 3)
            split_g_hi(1, 1, 1)
            transposed(1, 3)
            split_w_hi(1, 2)

            def pair(b):
                n = 2 * b
                project(b + 1, 0)
                project(b + 1, 1, ps_t)
                hidden_tanh(n, 0)
                logits_out(b)
                exponentials(b + 1, 0)
                split_g_hi(n, 0, 0)
                squares(b + 1, 0)
                exponentials(b + 1, 1)
                router_tanh(b)
                normed(b + 1, 0)
                hidden_tanh(n, 1)
                squares(b + 1, 1)
                transposed(b + 1, 0)
                split_g_hi(n, 0, 1)
                normed(b + 1, 1)
                exponentials(b + 1, 2)
                transposed(b + 1, 1)
                squares(b + 1, 2)
                normed(b + 1, 2)
                hidden_tanh(n + 1, 0)
                exponentials(b + 1, 3)
                split_g_hi(n + 1, 1, 0)
                transposed(b + 1, 2)
                squares(b + 1, 3)
                hidden_tanh(n + 1, 1)
                normed(b + 1, 3)
                split_g_hi(n + 1, 1, 1)
                transposed(b + 1, 3)

            with act.Fori(1, B - 1) as b:
                pair(b)

            def hidden(n, par):
                hidden_tanh(n, 0)
                split_g_hi(n, par, 0)
                hidden_tanh(n, 1)
                split_g_hi(n, par, 1)

            n = 2 * (B - 1)
            hidden_tanh(n, 0)
            logits_out(B - 1)
            split_g_hi(n, 0, 0)
            hidden_tanh(n, 1)
            router_tanh(B - 1)
            split_g_hi(n, 0, 1)
            hidden(n + 1, 1)
            with act.Fori(B, B * E // 2) as u:
                hidden(2 * u, 0)
                hidden(2 * u + 1, 1)

        @block.vector
        def _(dve):
            def wait_apart(done, value):
                dve.wait_ge(done, value)
                if not isinstance(value, int):
                    dve.sem_inc(s_apart_dve, 1)

            def key_mask_row(b):
                if isinstance(b, int) and b < 1:
                    dve.wait_ge(s_masks_in, 32)
                else:
                    dve.wait_ge(s_neg, NT * b)
                dve.tensor_scalar(key_neg[:], key_u8[:, ds(b * S, S)], MASKED, None,
                                  ALU.mult).then_inc(s_key_neg, 1)

            def first_stats(b):
                wait_apart(s_x_in, 16 * b)
                for t in range(NT):
                    dve.bn_stats(bn1[:, t, :], acc[:, ds((b * NT + t) * D, D)]).then_inc(s_bn1, 1)
                first_variance(b)

            def first_variance(b, a=0, z=NT):
                for t in range(a, z):
                    wait_apart(s_bn1, b * NT + t + 1)
                    dve.bn_aggr(mv1[:, t, :], bn1[:, t, :]).then_inc(s_mv1, 1)
                dve.wait_ge(s_mv1, NT * b + z)
                dve.tensor_scalar(ve1[:, a:z], mv1[:, a:z, 1], EPS, None, ALU.add).then_inc(s_ve1, 1)

            def batch0_stats(t):
                dve.wait_ge(s_x0_in[t], 16)
                dve.bn_stats(bn1[:, t, :], acc[:, t * D:(t + 1) * D]).then_inc(s_bn1, 1)

            def first_scale(b, a=0, z=NT):
                dve.wait_ge(s_rstd1, scale_count(b, z - 1))
                dve.tensor_scalar(rs1[:, a:z], rstd1[:, a:z], SCALING, None, ALU.mult).then_inc(s_rs1, 1)

            def weighted_scores(b, t, bank=ps_s):
                tile = b * NT + t
                dve.wait_ge(s_scores, tile + 1)
                if not (isinstance(b, int) and b == 0):
                    dve.wait_ge(s_sq, tile - 1)
                dve.scalar_tensor_tensor(out=row_buffer(b, t), in0=acc[:, ds(tile * D, D)],
                                         scalar=mv1[:, t, 0:1], in1=bank[:], op0=ALU.subtract,
                                         op1=ALU.mult).then_inc(s_z, 1)

            def row_maximum(b, t):
                tile = b * NT + t
                dve.wait_ge(s_z, tile + 1)
                wait_apart(s_neg, tile + 1)
                dve.tensor_tensor_reduce(row_buffer(b, t), row_buffer(b, t), neg[:, t % 2, :], 1.0, LOWEST,
                                         ALU.add, ALU.max, zmax[:, t:t + 1]).then_inc(s_zmax, 1)

            def masked_scores(b, t, bank=ps_s):
                weighted_scores(b, t, bank)
                row_maximum(b, t)

            def bias(b, t):
                dve.wait_ge(s_zmax, b * NT + t + 1)
                dve.wait_ge(s_rs1, scale_count(b, t))
                dve.scalar_tensor_tensor(out=nbias[:, t:t + 1], in0=zmax[:, t:t + 1], scalar=-1.0,
                                         in1=rs1[:, t:t + 1], op0=ALU.mult, op1=ALU.mult).then_inc(s_nb, 1)

            def scores(b, t, bank=ps_s):
                masked_scores(b, t, bank)
                bias(b, t)

            def split_w(e, part):
                a, z = 2 * part, 2 * part + 2
                dve.wait_ge(s_w_in[part], 16 * (e + 1))
                dve.tensor_copy(w_hi[:, e, a:z, :], w_raw[:, a:z, :]).then_inc(s_whi01, 1)
                dve.wait_ge(s_whi01, 2 * e + part + 1)
                dve.tensor_tensor(w_lo[:, e, a:z, :], w_raw[:, a:z, :], w_hi[:, e, a:z, :].bitcast(F32),
                                  ALU.subtract).then_inc(s_wlo01, 1)

            def inverse_sum(b, t):
                dve.wait_ge(s_exp, b * NT + t + 1)
                dve.reciprocal(rden[:, t:t + 1], psum_row[:, t:t + 1]).then_inc(s_rden, 1)

            def row_gain(b, t):
                dve.wait_ge(s_rden, b * NT + t + 1)
                dve.tensor_scalar(rgain[:, t:t + 1], rden[:, t:t + 1], tg[:, 0:1], None,
                                  ALU.mult).then_inc(s_rgain, 1)

            def add_attention(b, t):
                tile = b * NT + t
                row = acc[:, ds(tile * D, D)]
                dve.wait_ge(s_rgain, tile + 1)
                dve.scalar_tensor_tensor(out=row, in0=row_buffer(b, t), scalar=rgain[:, t:t + 1], in1=row,
                                         op0=ALU.mult, op1=ALU.add,
                                         accum_out=sum2[:, t:t + 1]).then_inc(s_x1, 1)

            def minus_mean(b, t):
                dve.wait_ge(s_x1, b * NT + t + 1)
                dve.tensor_scalar(nmean2[:, t:t + 1], sum2[:, t:t + 1], -1.0 / D, None,
                                  ALU.mult).then_inc(s_nmean, 1)

            def residual(b, t):
                inverse_sum(b, t)
                row_gain(b, t)
                add_attention(b, t)
                minus_mean(b, t)

            def split_wg():
                dve.wait_ge(s_wg_in, 16)
                dve.tensor_copy(wg_split[:, :, 0, :], wg_sb[:]).then_inc(s_wg_hi, 1)
                dve.wait_ge(s_wg_hi, 1)
                dve.tensor_tensor(wg_split[:, :, 1, :], wg_sb[:], wg_split[:, :, 0, :].bitcast(F32),
                                  ALU.subtract).then_inc(s_wg_lo, 1)

            def router_step(b, step, instruction):
                instruction.then_inc(s_rt, 1)
                dve.wait_ge(s_rt, b * RT + step)

            def router_ranks(b):
                full = [P, NT, E, E]
                gate_bias = gb_sb[:, 2:2 + E].unsqueeze(1).to_broadcast([P, NT, E])
                other = sc[:].unsqueeze(2).to_broadcast(full)
                own = sc[:].unsqueeze(3).to_broadcast(full)
                dve.wait_ge(s_lt, b + 1)
                router_step(b, 1, dve.tensor_scalar(sig[:], sig[:], 0.5, 0.5, ALU.mult, ALU.add))
                router_step(b, 2, dve.tensor_tensor(sc[:], sig[:], gate_bias, ALU.add))
                router_step(b, 3, dve.tensor_tensor(above[:], other, own, ALU.is_gt))
                router_step(b, 4, dve.tensor_tensor(ties[:], other, own, ALU.is_equal))
                router_step(b, 5, dve.tensor_tensor(ties[:], ties[:], before[:].unsqueeze(1).to_broadcast(full),
                                                    ALU.mult))
                router_step(b, 6, dve.tensor_tensor(above[:], above[:], ties[:], ALU.add))
                router_step(b, 7, dve.tensor_reduce(rank[:], above[:], AX_X, ALU.add))

            def router_weights(b):
                router_step(b, 8, dve.scalar_tensor_tensor(out=picked[:], in0=rank[:], scalar=float(TOP_K),
                                                           in1=sig[:], op0=ALU.is_lt, op1=ALU.mult))
                router_step(b, 9, dve.tensor_reduce(wsum[:], picked[:], AX_X, ALU.add))
                router_step(b, RT, dve.reciprocal(wrec[:], wsum[:]))
                dve.scalar_tensor_tensor(out=wts[:, ds(b * (NT * E), NT * E)].rearrange("p (t e) -> p t e", t=NT),
                                         in0=picked[:], scalar=half_gain[:],
                                         in1=wrec[:].unsqueeze(2).to_broadcast([P, NT, E]),
                                         op0=ALU.mult, op1=ALU.mult).then_inc(s_wts, 1)

            def router(b):
                router_ranks(b)
                router_weights(b)

            def gated(n, c):
                k = n * FC + c
                dve.wait_ge(s_th, k + 1)
                if not (isinstance(k, int) and k < FC):
                    dve.wait_ge(s_glo, k - FC + 1)
                dve.scalar_tensor_tensor(out=gate[:, c, :], in0=th[:, c, :], scalar=1.0, in1=ps_h[0][c][:],
                                         op0=ALU.add, op1=ALU.mult).then_inc(s_gate, 1)

            def times_h3(n, c):
                k = n * FC + c
                dve.wait_ge(s_h3, k + 1)
                dve.wait_ge(s_gate, k + 1)
                dve.tensor_tensor(gate[:, c, :], gate[:, c, :], ps_h[1][c][:], ALU.mult).then_inc(s_prod, 1)

            def add_output(n, e, g, t):
                dve.wait_ge(s_o, n * NT + t + 1)
                row = acc[:, ds((g * NT + t) * D, D)]
                dve.scalar_tensor_tensor(out=row, in0=ps_o[t % 2][:],
                                         scalar=wts[:, ds((g * NT + t) * E + e, 1)], in1=row,
                                         op0=ALU.mult, op1=ALU.add).then_inc(s_acc, 1)

            batch0_stats(0)
            first_variance(0, 0, 1)
            key_mask_row(0)
            batch0_stats(1)
            batch0_stats(2)
            weighted_scores(0, 0, first_s[0])
            first_scale(0, 0, 1)
            row_maximum(0, 0)
            bias(0, 0)
            batch0_stats(3)
            first_variance(0, 1, NT)
            weighted_scores(0, 1, first_s[1])
            dve.wait_ge(s_tg, 1)
            dve.tensor_scalar(half_gain[:], tg[:, 1:2], 0.5, None, ALU.mult).then_inc(s_hg, 1)
            inverse_sum(0, 0)
            row_gain(0, 0)
            first_scale(0, 1, NT)
            add_attention(0, 0)
            minus_mean(0, 0)
            row_maximum(0, 1)
            bias(0, 1)
            weighted_scores(0, 2, first_s[2])
            inverse_sum(0, 1)
            row_gain(0, 1)
            row_maximum(0, 2)
            bias(0, 2)
            add_attention(0, 1)
            minus_mean(0, 1)
            weighted_scores(0, 3, first_s[3])
            inverse_sum(0, 2)
            row_gain(0, 2)
            row_maximum(0, 3)
            bias(0, 3)
            add_attention(0, 2)
            minus_mean(0, 2)
            residual(0, 3)
            split_w(0, 0)
            split_w(0, 1)
            split_wg()
            key_mask_row(1)
            first_stats(1)
            first_scale(1)
            split_w(1, 0)
            dve.wait_ge(s_hg, 1)
            dve.wait_ge(s_ident, 2)

            dve.wait_ge(s_xlo, 3)
            scores(1, 0)
            split_w(1, 1)
            gated(0, 0)
            scores(1, 1, ps_t)
            times_h3(0, 0)
            residual(1, 0)
            gated(0, 1)
            residual(1, 1)
            scores(1, 2)
            times_h3(0, 1)
            router_ranks(0)
            scores(1, 3)
            residual(1, 2)
            gated(1, 0)
            times_h3(1, 0)
            router_weights(0)
            residual(1, 3)
            gated(1, 1)
            dve.wait_ge(s_wts, 1)
            add_output(0, 0, 0, 0)
            times_h3(1, 1)
            add_output(0, 0, 0, 1)
            add_output(0, 0, 0, 2)
            add_output(0, 0, 0, 3)

            def pair(b):
                n = 2 * b
                key_mask_row(b + 1)
                first_stats(b + 1)
                gated(n, 0)
                masked_scores(b + 1, 0)
                first_scale(b + 1)
                bias(b + 1, 0)
                times_h3(n, 0)
                residual(b + 1, 0)
                scores(b + 1, 1)
                gated(n, 1)
                residual(b + 1, 1)
                times_h3(n, 1)
                add_output(n - 1, 1, b - 1, 0)
                add_output(n - 1, 1, b - 1, 1)
                scores(b + 1, 2)
                add_output(n - 1, 1, b - 1, 2)
                residual(b + 1, 2)
                add_output(n - 1, 1, b - 1, 3)
                router(b)
                gated(n + 1, 0)
                scores(b + 1, 3)
                times_h3(n + 1, 0)
                residual(b + 1, 3)
                gated(n + 1, 1)
                times_h3(n + 1, 1)
                dve.wait_ge(s_wts, b + 1)
                for t in range(NT - 1):
                    add_output(n, 0, b, t)
                add_output(n, 0, b, NT - 1)

            with dve.Fori(1, B - 1) as b:
                pair(b)

            def unit(n, prev_n, prev_e, prev_g):
                for c in range(FC):
                    gated(n, c)
                    times_h3(n, c)
                for t in range(NT):
                    add_output(prev_n, prev_e, prev_g, t)

            unit(2 * B - 2, 2 * B - 3, 1, B - 2)
            router(B - 1)
            dve.wait_ge(s_wts, B)
            unit(2 * B - 1, 2 * B - 2, 0, B - 1)
            unit(2 * B, 2 * B - 1, 1, B - 1)
            unit(2 * B + 1, 2 * B, 2, 0)
            unit(2 * B + 2, 2 * B + 1, 2, 1)
            unit(2 * B + 3, 2 * B + 2, 2, 2)
            with dve.Fori(3, E) as e:
                unit(B * e, B * e - 1, e - 1, B - 1)
                with dve.Fori(1, B) as g:
                    unit(B * e + g, B * e + g - 1, e, g - 1)
            for t in range(NT):
                add_output(LAST, E - 1, B - 1, t)

        @block.tensor
        def _(pe):
            def project(b, i, bank=ps_s):
                pe.wait_ge(s_ctx_in, 16 * (b + 1))
                if i == 0 and not (isinstance(b, int) and b == 0):
                    pe.wait_ge(s_z, NT * b)
                pe.matmul(bank[:], wqk_sb[:, i * P:(i + 1) * P], ctx_sb[:], start=True,
                          stop=True).then_inc(s_proj, 1)

            def scores(b, t, bank=ps_s, skipped=0):
                pe.wait_ge(s_qk, 2 * b + 2)
                if t > 0 and bank is ps_s and not (isinstance(b, int) and b == 0):
                    pe.wait_ge(s_z, b * NT + t - skipped)
                pe.matmul(bank[:], q_sb[:, t * P:(t + 1) * P], k_sb[:], start=True,
                          stop=True).then_inc(s_scores, 1)

            def transpose(b, t, bank=ps_t):
                tile = b * NT + t
                pe.wait_ge(s_xn, tile + 1)
                if t == 0 and not (isinstance(b, int) and b < 2):
                    pe.wait_ge(s_lt, b)
                elif t > 0 and not (isinstance(b, int) and b == 0):
                    pe.wait_ge(s_xhi, tile)
                for k in range(KC):
                    mm = pe.transpose(bank[:, k * P:(k + 1) * P], xn[:, k * P:(k + 1) * P], ident[:])
                mm.then_inc(s_xpose, 1)

            def both_parts_logits(b, bank=ps_t):
                for k in range(KC):
                    for part, x_part in enumerate((xt_hi, xt_lo)):
                        mm = pe.matmul(bank[0:2 * E, :], wg_split[:, k].rearrange("p h e -> p (h e)"),
                                       x_part[:, ds(b * GRP + k * S, S)], start=(k == 0 and part == 0),
                                       stop=(k == KC - 1 and part == 1))
                mm.then_inc(s_both_logits, 1)

            def logits(b, bank=ps_t):
                pe.wait_ge(s_logits_out, b + 1)
                for t in range(NT):
                    mm = pe.matmul(bank[:, t * E:(t + 1) * E], both_logits[:, t * P:(t + 1) * P],
                                   add_parts[0:2 * E, :], start=True, stop=True)
                mm.then_inc(s_logits, 1)

            def hidden(n, slot, g, c, m, half=None):
                kk = n * FC + c
                if not (isinstance(n, int) and n == 0):
                    pe.wait_ge((s_gate, s_prod)[m], kk - FC + 1)
                a, size = (0, S) if half is None else (half * (S // 2), S // 2)
                bank = ps_h[m][c][:, a:a + size]
                for k in range(KC):
                    w = slice(k * P, (k + 1) * P)
                    hi = w_hi[:, slot, 2 * c + m, w]
                    lo = w_lo[:, slot, 2 * c + m, w]
                    x_hi = xt_hi[:, ds(g * GRP + (k * S + a), size)]
                    x_lo = xt_lo[:, ds(g * GRP + (k * S + a), size)]
                    pe.matmul(bank, hi, x_hi, start=(k == 0), stop=False)
                    pe.matmul(bank, hi, x_lo, start=False, stop=False)
                    mm = pe.matmul(bank, lo, x_hi, start=False, stop=(k == KC - 1))
                mm.then_inc((s_h1, s_h3)[m], 1)

            def first_hidden(t, c, m):
                if t == 0 and m == 0:
                    pe.wait_ge(s_w_in[c], 16)
                if c == 0 and m == 0:
                    pe.wait_ge(s_xt32, t + 1)
                for k in range(KC):
                    mm = pe.matmul(ps_h[m][c][:, t * P:(t + 1) * P], w_raw[:, 2 * c + m, k * P:(k + 1) * P],
                                   transposed_f32(0, t)[:, k, :], start=(k == 0), stop=(k == KC - 1))
                if t == 1 and m == 1:
                    mm.then_inc(s_first, 1)

            def keep_clock(count):
                for i in range(count):
                    pe.matmul(ps_h[1][1][:, 0:P], ident[:], ident[:], start=True, stop=True)

            def output(n, par, slot, t):
                if t == 0:
                    pe.wait_ge(s_ghi, FC * (n + 1))
                    pe.wait_ge(s_glo, FC * (n + 1))
                if not (isinstance(n, int) and n == 0 and t < 2):
                    pe.wait_ge(s_acc, n * NT + t - 1)
                bank = ps_o[t % 2]
                tok = slice(t * P, (t + 1) * P)
                for c in range(FC):
                    pe.matmul(bank[:], g_hi[:, par, c, tok], w_hi[:, slot, 2 * FC + c, :],
                              start=(c == 0), stop=False)
                    pe.matmul(bank[:], g_hi[:, par, c, tok], w_lo[:, slot, 2 * FC + c, :],
                              start=False, stop=False)
                    mm = pe.matmul(bank[:], g_lo[:, par, c, tok], w_hi[:, slot, 2 * FC + c, :],
                                   start=False, stop=(c == FC - 1))
                mm.then_inc(s_o, 1)

            pe.wait_ge(s_ident, 2)
            pe.wait_ge(s_wqk_in, 16)
            project(0, 0)
            project(0, 1, ps_o[0])
            scores(0, 0, first_s[0])
            scores(0, 1, first_s[1])
            scores(0, 2, first_s[2])
            pe.wait_ge(s_z, 1)
            scores(0, 3, first_s[3])
            keep_clock(WARM[0])
            transpose(0, 0)
            keep_clock(WARM[1])
            first_hidden(0, 0, 0)
            first_hidden(0, 0, 1)
            first_hidden(0, 1, 0)
            transpose(0, 1, first_t[1])
            first_hidden(0, 1, 1)
            first_hidden(1, 0, 0)
            first_hidden(1, 0, 1)
            transpose(0, 2, first_t[2])
            pe.wait_ge(s_xhi, 2)
            project(1, 0)
            project(1, 1, ps_t)
            first_hidden(1, 1, 0)
            first_hidden(1, 1, 1)
            transpose(0, 3, first_t[3])
            scores(1, 0)
            scores(1, 1, ps_t)

            pe.wait_ge(s_wlo01, 2)
            pe.wait_ge(s_xlo, 4)
            hidden(0, 0, 0, 0, 0, half=1)
            hidden(0, 0, 0, 0, 1, half=1)
            pe.wait_ge(s_wg_lo, 1)
            both_parts_logits(0, ps_o[0])
            hidden(0, 0, 0, 1, 0, half=1)
            hidden(0, 0, 0, 1, 1, half=1)
            pe.wait_ge(s_wlo01, 3)
            hidden(1, 1, 0, 0, 0)
            pe.wait_ge(s_ident, 4)
            logits(0, ps_o[0])
            scores(1, 2, skipped=1)
            pe.wait_ge(s_z, NT + 2)
            transpose(1, 0)
            hidden(1, 1, 0, 0, 1)
            scores(1, 3)
            pe.wait_ge(s_wlo01, 4)
            hidden(1, 1, 0, 1, 0)
            transpose(1, 1)
            hidden(1, 1, 0, 1, 1)
            pe.wait_ge(s_lt, 1)
            pe.wait_ge(s_wlo, split_count(0, 2))
            output(0, 0, 0, 0)
            output(0, 0, 0, 1)
            transpose(1, 2)
            output(0, 0, 0, 2)
            transpose(1, 3)
            output(0, 0, 0, 3)

            def pair(b):
                n = 2 * b
                project(b + 1, 0)
                pe.wait_ge(s_xhi, NT * (b + 1))
                project(b + 1, 1, ps_t)
                pe.wait_ge(s_xlo, NT * (b + 1))
                hidden(n, 0, b, 0, 0)
                scores(b + 1, 0)
                both_parts_logits(b)
                hidden(n, 0, b, 0, 1)
                scores(b + 1, 1)
                hidden(n, 0, b, 1, 0)
                logits(b)
                hidden(n, 0, b, 1, 1)
                pe.wait_ge(s_wlo, split_count(1, 2))
                output(n - 1, 1, 1, 0)
                transpose(b + 1, 0)
                output(n - 1, 1, 1, 1)
                scores(b + 1, 2)
                output(n - 1, 1, 1, 2)
                transpose(b + 1, 1)
                output(n - 1, 1, 1, 3)
                hidden(n + 1, 1, b, 0, 0)
                scores(b + 1, 3)
                hidden(n + 1, 1, b, 0, 1)
                transpose(b + 1, 2)
                hidden(n + 1, 1, b, 1, 0)
                hidden(n + 1, 1, b, 1, 1)
                output(n, 0, 0, 0)
                output(n, 0, 0, 1)
                transpose(b + 1, 3)
                output(n, 0, 0, 2)
                output(n, 0, 0, 3)

            with pe.Fori(1, B - 1) as b:
                pair(b)
            pe.wait_ge(s_xhi, NT * B)
            pe.wait_ge(s_xlo, NT * B)

            def unit(n, slot, g, prev_n, prev_par, prev_slot):
                for c in range(FC):
                    hidden(n, slot, g, c, 0)
                    hidden(n, slot, g, c, 1)
                for t in range(NT):
                    output(prev_n, prev_par, prev_slot, t)

            hidden(2 * B - 2, 0, B - 1, 0, 0)
            hidden(2 * B - 2, 0, B - 1, 0, 1)
            both_parts_logits(B - 1)
            hidden(2 * B - 2, 0, B - 1, 1, 0)
            hidden(2 * B - 2, 0, B - 1, 1, 1)
            logits(B - 1)
            for t in range(NT):
                output(2 * B - 3, 1, 1, t)
            unit(2 * B - 1, 1, B - 1, 2 * B - 2, 0, 0)
            with pe.Fori(1, E // 2) as p:
                for slot in range(2):
                    n = p * (2 * B) + slot * B
                    pe.wait_ge(s_wlo, split_count(p * 2 + slot, 1))
                    unit(n, slot, 0, n - 1, 1, 1 - slot)
                    pe.wait_ge(s_wlo, split_count(p * 2 + slot, 2))
                    unit(n + 1, slot, 1, n, 0, slot)
                    unit(n + 2, slot, 2, n + 1, 1, slot)
                    unit(n + 3, slot, 3, n + 2, 0, slot)
            for t in range(NT):
                output(LAST, 1, 1, t)


def kernel(x, ctx_512, mask_SxS2_bk1, mask_BxS2_bf0, g_xattn, g_ffn, L0_xattn_Wq, L0_xattn_bq, L0_xattn_Wk,
           L0_xattn_bk, L0_ffn_Wg, L0_ffn_W1, L0_ffn_W2, L0_ffn_W3, L0_ffn_bias):
    import numpy as np
    import concourse.bacc as bacc
    from concourse.bass_utils import run_bass_kernel_spmd

    x = np.asarray(x)
    B, S, D = x.shape
    E, F, _ = L0_ffn_W1.shape
    fc, kc = F // P, D // P

    def hidden_layout(w):
        w = np.asarray(w).reshape(E, fc, P, kc, P).transpose(0, 4, 1, 3, 2)
        return w.reshape(E, P, fc, 1, D)

    w13 = np.concatenate([hidden_layout(L0_ffn_W1), hidden_layout(L0_ffn_W3)], axis=3).reshape(E, P, 2 * fc, D)
    w2 = np.asarray(L0_ffn_W2).reshape(E, D, fc, P).transpose(0, 3, 2, 1)
    arrays = {
        "x": x,
        "ctx_t": np.asarray(ctx_512).transpose(0, 2, 1),
        "wqk_t": np.concatenate([np.asarray(L0_xattn_Wq).T, np.asarray(L0_xattn_Wk).T], axis=1),
        "bqk": np.stack([np.asarray(L0_xattn_bq), np.asarray(L0_xattn_bk)], axis=1),
        "gains_bias": np.concatenate([np.asarray(g_xattn), np.asarray(g_ffn), np.asarray(L0_ffn_bias)]),
        "attn_mask": np.asarray(mask_SxS2_bk1),
        "key_mask": np.asarray(mask_BxS2_bf0).reshape(-1),
        "wg_t": np.asarray(L0_ffn_Wg).reshape(E, kc, P).transpose(2, 1, 0),
        "experts": np.concatenate([w13, w2], axis=2),
    }
    arrays = {f"in_{n}": np.ascontiguousarray(a) for n, a in arrays.items()}
    nc = bacc.Bacc("TRN2", target_bir_lowering=False, num_devices=1)
    ins = [nc.dram_tensor(n, a.shape, mybir.dt.from_np(a.dtype), kind="ExternalInput").ap()
           for n, a in arrays.items()]
    out = nc.dram_tensor("out", (B * S // P, P, D), F32, kind="ExternalOutput").ap()
    flamingo_gated_block(nc, *ins, out)
    r = run_bass_kernel_spmd(nc, [arrays], core_ids=[0])
    return r.results[0]["out"].reshape(B, S, D)
```
